# Optimizing a Trainium2 kernel written in Bass

```python
import numpy as np
import jax
import jax.numpy as jnp

def _softmax(x, axis=-1):
    return jax.nn.softmax(x, axis=axis)
def _gelu(x):
    return jax.nn.gelu(x, approximate=True)
def _silu(x):
    return jax.nn.silu(x)
def _sigmoid(x):
    return jax.nn.sigmoid(x)
def _layernorm(x, axis=-1, eps=1e-5):
    m = jnp.mean(x, axis=axis, keepdims=True)
    v = jnp.var(x, axis=axis, keepdims=True)
    return (x - m) / jnp.sqrt(v + eps)
def _scatter_add(tgt, idx, src, axis=0):
    return tgt.at[idx].add(src)
def _segment_sum(src, seg, n):
    return jax.ops.segment_sum(src, seg, n)

kernel_name = 'mk_conv_seq_d1_conv_nhwc96_fe286c'

def setup_inputs(seed: int = 0):
    np.random.seed(seed)
    _w = jnp.asarray
    def _rec_inputs():
        import jax
        import jax.numpy as jnp
        _gk = jax.random.key(seed)
        x = -9.26e-05 + 0.9999 * jax.random.normal(jax.random.fold_in(_gk, 1), (8, 512, 96, 96), jnp.float32)
        return x
    x = _rec_inputs()
    def _L0_conv_setup():
        import jax, jax.numpy as jnp
        import numpy as np
        B, C, H, W = (8, 512, 96, 96)
        CQ = C // 8
        NEG = jnp.float32(1e+30)
        ks = jax.random.split(jax.random.key(seed), 8)
        s = 0.05
        return {'x': jax.random.normal(ks[0], (B, C, H, W), jnp.float32), 'Wq': jax.random.normal(ks[1], (CQ, C), jnp.float32) * s, 'bq': jnp.zeros((CQ,), jnp.float32), 'Wk': jax.random.normal(ks[2], (CQ, C), jnp.float32) * s, 'bk': jnp.zeros((CQ,), jnp.float32), 'Wv': jax.random.normal(ks[3], (C, C), jnp.float32) * s, 'bv': jnp.zeros((C,), jnp.float32), 'gamma': jnp.full((1,), 0.1, jnp.float32)}
    _L0_conv_all = _L0_conv_setup()
    _L0_conv_in = {k: v for k, v in _L0_conv_all.items() if k in ('Wq', 'bq', 'Wk', 'bk', 'Wv', 'bv', 'gamma', )}
    del _L0_conv_all

    return {
        "x": x,
        "L0_conv_Wq": _L0_conv_in["Wq"],
        "L0_conv_bq": _L0_conv_in["bq"],
        "L0_conv_Wk": _L0_conv_in["Wk"],
        "L0_conv_bk": _L0_conv_in["bk"],
        "L0_conv_Wv": _L0_conv_in["Wv"],
        "L0_conv_bv": _L0_conv_in["bv"],
        "L0_conv_gamma": _L0_conv_in["gamma"],
    }

def reference(x, L0_conv_Wq, L0_conv_bq, L0_conv_Wk, L0_conv_bk, L0_conv_Wv, L0_conv_bv, L0_conv_gamma):
    import jax
    import jax.numpy as jnp
    def _L0_conv_ref(x, Wq, bq, Wk, bk, Wv, bv, gamma):
        import jax, jax.numpy as jnp
        import numpy as np
        B, C, H, W = (8, 512, 96, 96)
        CQ = C // 8
        NEG = jnp.float32(1e+30)
        q = jnp.einsum('oc,bchw->bohw', Wq, x) + bq[None, :, None, None]
        k = jnp.einsum('oc,bchw->bohw', Wk, x) + bk[None, :, None, None]
        v = jnp.einsum('oc,bchw->bohw', Wv, x) + bv[None, :, None, None]
        energy_H = jnp.einsum('bchw,bcgw->bhwg', q, k)
        eye = jnp.eye(H, dtype=x.dtype)
        energy_H = energy_H - NEG * eye[None, :, None, :]
        energy_W = jnp.einsum('bchw,bchv->bhwv', q, k)
        att = jax.nn.softmax(jnp.concatenate([energy_H, energy_W], axis=-1), axis=-1)
        att_H, att_W = (att[..., :H], att[..., H:])
        out_H = jnp.einsum('bcgw,bhwg->bchw', v, att_H)
        out_W = jnp.einsum('bchv,bhwv->bchw', v, att_W)
        return gamma * (out_H + out_W) + x

    def _gn(v, G=32, eps=1e-5):
        B_, H_, W_, C_ = v.shape
        g = v.reshape(B_, H_, W_, G, C_ // G)
        m = jnp.mean(g, axis=(1, 2, 4), keepdims=True)
        s = jnp.var(g, axis=(1, 2, 4), keepdims=True)
        return ((g - m) / jnp.sqrt(s + eps)).reshape(v.shape)

    def _ln_c(v, eps=1e-6):
        m = jnp.mean(v, axis=-1, keepdims=True)
        s = jnp.var(v, axis=-1, keepdims=True)
        return (v - m) / jnp.sqrt(s + eps)

    def _ln_t(v, eps=1e-5):
        m = jnp.mean(v, axis=-1, keepdims=True)
        s = jnp.var(v, axis=-1, keepdims=True)
        return (v - m) / jnp.sqrt(s + eps)

    def _to_tokens(v):
        B_, H_, W_, C_ = v.shape
        return v.reshape(B_, H_ * W_, C_)
    def _from_tokens(t, like):
        return t.reshape(like.shape)

    x = _L0_conv_ref(x, L0_conv_Wq, L0_conv_bq, L0_conv_Wk, L0_conv_bk, L0_conv_Wv, L0_conv_bv, L0_conv_gamma)
    return x


_drawn_inputs = setup_inputs


def setup_inputs(seed=0):
    import zlib

    import numpy as np

    out = dict(_drawn_inputs(seed))
    spreads = {'L0_conv_bq': (0.0, 0.321), 'L0_conv_bk': (0.0, 0.8), 'L0_conv_bv': (0.0, 0.8)}
    factors = {}
    for name, (base, spread) in spreads.items():
        noise = np.random.default_rng([zlib.crc32(name.encode()), seed]).standard_normal(out[name].shape)
        drawn = base * np.exp(spread * noise) if base else spread * noise
        out[name] = jnp.asarray(drawn.astype(out[name].dtype))
    for name, factor in factors.items():
        out[name] = (out[name] * factor).astype(out[name].dtype)
    return out
```

```python
from contextlib import ExitStack

import concourse.bass as bass
from concourse import mybir

ALU = mybir.AluOpType
ACT = mybir.ActivationFunctionType
AX_X = mybir.AxisListType.X
F32 = mybir.dt.float32
F32R = mybir.dt.float32r

P = 128
N = 96
POS = N * N
ROWS = 4
CP = ROWS * N
CHUNKS = N // ROWS
PAIRS = CHUNKS // 2
TILES = CP // P
SUB = 2
SP_ = SUB * N
SUBS = N // SUB
ERING = 4
MASKED = -1e30


def criss_cross_attention(nc, x, wqk_t, wv_t, bqk, bv, gamma, out):
    B, C = x.shape[0], x.shape[1]
    CT = C // P
    CQ = wqk_t.shape[1] // 2
    assert x.shape[2] == N and x.shape[3] == N and C % P == 0 and 2 * CQ == P and CP % P == 0

    v_dram = nc.dram_tensor("v_scratch", (B, POS, C), F32, kind="Internal").ap()
    kq_dram = nc.dram_tensor("kq_scratch", (B, 2, CQ, POS), F32, kind="Internal").ap()
    e_dram = nc.dram_tensor("e_scratch", (2, B, N, N, N), F32, kind="Internal").ap()

    x_v = x.rearrange("b (t p) h w -> b p t (h w)", p=P)
    out_v = out.rearrange("b (t p) h w -> b p t (h w)", p=P)
    v_by_column = v_dram.rearrange("b (g w) c -> b g w c", g=N)
    v_by_row = v_dram.rearrange("b (h u) c -> b u h c", h=N)

    ctx = ExitStack()
    with ctx:
        def sb(name, shape, dt=F32, at=None):
            return (at or ctx).enter_context(nc.sbuf_tensor(name, shape, dt))

        def sem(name):
            return ctx.enter_context(nc.semaphore(name))

        X = sb("X", [P, CT, POS])
        Wv_hi = sb("Wv_hi", [P, CT, C], F32R)
        Wv_lo = sb("Wv_lo", [P, CT, C], F32R)
        Wqk_hi = sb("Wqk_hi", [P, CT, P], F32R)
        Wqk_lo = sb("Wqk_lo", [P, CT, P], F32R)
        ident = sb("ident", [N, N])
        mask = sb("mask", [N, N])
        bqk_sb = sb("bqk_sb", [P, 1])
        gamma_sb = sb("gamma_sb", [P, 1])
        kq = sb("kq", [P, 2, SP_])
        E = sb("E", [N, ERING, SUB, N])
        mx = sb("mx", [N, 2, N])
        zs = sb("zs", [N, 2, N])
        with ExitStack() as s1:
            x_hi = sb("x_hi", [P, 2, CT, CP], F32R, s1)
            x_lo = sb("x_lo", [P, 2, CT, CP], F32R, s1)
            v_out = sb("v_out", [P, 2, C], F32, s1)
            bv_row = sb("bv_row", [P, C], F32, s1)
        with ExitStack() as s2:
            KQ = sb("KQ", [P, POS], F32, s2)
        with ExitStack() as s3:
            V = sb("V", [P, 2, ROWS, C], F32, s3)
            Pe = sb("Pe", [N, 2, ROWS, N], F32, s3)
            Pt = sb("Pt", [P, 2, ROWS, N], F32, s3)
            st = sb("st", [N, 4, N], F32, s3)

        bank = [ctx.enter_context(nc.psum_tensor(f"bank{i}", [P, 512], F32)) for i in range(8)]
        v_ps, kq_ps, e_ps, o_ps = bank[0:2], bank[2:4], bank[4:6], bank[6:8]
        t_ps = kq_ps

        consts_in = sem("consts_in")
        consts_made = sem("consts_made")
        kq_padded = sem("kq_padded")
        w_hi_made = sem("w_hi_made")
        w_lo_made = sem("w_lo_made")
        x_in = [sem(f"x_in{j}") for j in range(2)]
        bv_in = sem("bv_in")
        x_hi_made = sem("x_hi_made")
        x_lo_made = sem("x_lo_made")
        v_summed = sem("v_summed")
        v_evicted = sem("v_evicted")
        v_stored = [sem(f"v_stored{j}") for j in range(2)]
        kq_summed = sem("kq_summed")
        kq_evicted = sem("kq_evicted")
        kq_stored = sem("kq_stored")
        sync_stages = sem("sync_stages")
        kq_in = sem("kq_in")
        q_gathered = sem("q_gathered")
        e_summed = sem("e_summed")
        e_maxed = sem("e_maxed")
        e_shifted = sem("e_shifted")
        e_exped = sem("e_exped")
        z_summed = sem("z_summed")
        e_stored = [sem(f"e_stored{j}") for j in range(ERING)]
        st_turned = sem("st_turned")
        st_step = sem("st_step")
        st_exped = sem("st_exped")
        f_turned = sem("f_turned")
        f_made = sem("f_made")
        v_in = [sem(f"v_in{j}") for j in range(2)]
        p_in = [sem(f"p_in{j}") for j in range(2)]
        pads_made = sem("pads_made")
        p_scaled = sem("p_scaled")
        p_turned = sem("p_turned")
        pt_made = sem("pt_made")
        o_summed = sem("o_summed")
        o_added = sem("o_added")
        out_stored = [sem(f"out_stored{j}") for j in range(2)]

        def e_no(b, down, p, c):
            return b * (2 * SUBS) + SUBS * down + p * 4 + c

        def g_no(b, along, p, c):
            return b * (2 * CHUNKS) + CHUNKS * along + p * 2 + c

        block = ctx.enter_context(nc.Block())

        @block.sync
        def _(sp):
            sp.dma_start(X[:, 0, 0:CT * C].rearrange("p (t n) -> p t n", t=CT),
                         wv_t.rearrange("(t p) n -> p t n", p=P)).then_inc(consts_in, 16)
            sp.dma_start(X[:, 1, 0:CT * P].rearrange("p (t n) -> p t n", t=CT),
                         wqk_t.rearrange("(t p) n -> p t n", p=P)).then_inc(consts_in, 16)
            sp.dma_start(bqk_sb[:, :], bqk).then_inc(consts_in, 16)
            sp.dma_start(gamma_sb[:, :], gamma.to_broadcast((P, 1))).then_inc(consts_in, 16)
            sp.wait_ge(w_hi_made, 2)
            sp.wait_ge(w_lo_made, 2)

            def load_x(b, p, c):
                j, n = c % 2, p + c // 2
                sp.wait_ge(x_in[j], 16 * (b * PAIRS + n))
                at = bass.ds((p * 2 + c) * CP, CP)
                sp.dma_start(X[:, :, at], x_v[b, :, :, at]).then_inc(x_in[j], 16)

            def store_v(b, p, c, s):
                t = TILES * c + s
                sp.wait_ge(v_evicted, b * (TILES * CHUNKS) + p * (2 * TILES) + t + 1 + 2)
                sp.dma_start(v_dram[b, bass.ds(p * (2 * CP) + t * P, P), :], v_out[:, t % 2, :])\
                    .then_inc(v_stored[t % 2], 16)

            def store_kq(b, p, c, v):
                u = 2 * c + v
                sp.wait_ge(kq_evicted, b * SUBS + p * 4 + u + 1 + 2)
                sp.dma_start(kq_dram[b, :, :, bass.ds((p * 4 + u) * SP_, SP_)].rearrange("t c n -> c t n"),
                             kq[0:CQ, :, :]).then_inc(kq_stored, 16)

            def store_e(b, down, p, c):
                sp.wait_ge(e_exped, e_no(b, down, p, c) + 1)
                sp.dma_start(e_dram[1 - down, b, :, bass.ds((p * 4 + c) * SUB, SUB), :], E[:, c % ERING, :, :])\
                    .then_inc(e_stored[c % ERING], 16)

            def stores(b, p, c):
                store_v(b, p, c, 0)
                store_kq(b, p, c - 1, 0)
                store_v(b, p, c, 1)
                store_e(b, 0, p, 2 * (c - 1))
                store_kq(b, p, c - 1, 1)
                store_v(b, p, c, 2)
                store_e(b, 0, p, 2 * (c - 1) + 1)

            def load_attention(b, along, p, c, free=False):
                g = g_no(b, along, p, c)
                at = bass.ds((p * 2 + c) * ROWS, ROWS)
                if not free:
                    sp.wait_ge(p_turned, g)
                sp.dma_start(Pe[:, c % 2, :, :], e_dram[along, b, :, at, :]).then_inc(p_in[c % 2], 16)
                if not free:
                    sp.wait_ge(o_summed, g * ROWS)
                sp.dma_start(V[0:N, c % 2, :, :], (v_by_row if along else v_by_column)[b, :, at, :])\
                    .then_inc(v_in[c % 2], 16)

            def store_out(b, p, c):
                sp.wait_ge(o_added, (g_no(b, 1, p, c) + 1) * ROWS + 2)
                at = bass.ds((p * 2 + c) * CP, CP)
                sp.dma_start(out_v[b, :, :, at], X[:, :, at]).then_inc(out_stored[c % 2], 16)

            with sp.Fori(0, B) as b:
                for j in range(2):
                    sp.wait_ge(out_stored[j], b * (16 * PAIRS))
                for c in range(4):
                    load_x(b, 0, c)
                sp.dma_start(bv_row[:, :], bv.to_broadcast((P, C))).then_inc(bv_in, 16)
                for s in range(TILES):
                    store_v(b, 0, 0, s)
                with sp.Fori(0, PAIRS - 2) as p:
                    for c in (1, 2):
                        load_x(b, p, c + 3)
                        stores(b, p, c)
                for c in (1, 2, 3):
                    stores(b, PAIRS - 2, c)
                for v in range(2):
                    store_kq(b, PAIRS - 1, 1, v)
                    store_e(b, 0, PAIRS - 1, 2 + v)
                for j in range(2):
                    sp.wait_ge(v_stored[j], (b + 1) * (16 * TILES * CHUNKS // 2))
                sp.sem_inc(sync_stages, 1)
                sp.wait_ge(kq_stored, (b + 1) * (16 * SUBS))
                sp.sem_inc(sync_stages, 1)
                sp.dma_start(KQ[:, :], kq_dram[b].rearrange("t c n -> (t c) n")).then_inc(kq_in, 16)
                with sp.Fori(0, SUBS // 4) as p:
                    for c in range(4):
                        store_e(b, 1, p, c)
                for j in range(ERING):
                    sp.wait_ge(e_stored[j], (b + 1) * (16 * 2 * SUBS // ERING))
                sp.sem_inc(sync_stages, 1)
                for along in range(2):
                    if along:
                        load_attention(b, 1, 0, 0)
                        load_attention(b, 1, 0, 1)
                        with sp.Fori(0, PAIRS - 1) as p:
                            for c in range(2):
                                load_attention(b, 1, p, c + 2)
                                store_out(b, p, c)
                        store_out(b, PAIRS - 1, 0)
                        store_out(b, PAIRS - 1, 1)
                    else:
                        load_attention(b, 0, 0, 0, free=True)
                        load_attention(b, 0, 0, 1, free=True)
                        with sp.Fori(1, PAIRS) as p:
                            for c in range(2):
                                load_attention(b, 0, p, c)
            for j in range(2):
                sp.wait_ge(out_stored[j], 16 * PAIRS * B)

        @block.gpsimd
        def _(pool):
            nc.gpsimd.memset(ident[:, :], 0.0).then_inc(consts_made, 1)
            nc.gpsimd.memset(mask[:, :], 0.0).then_inc(consts_made, 1)
            pool.wait_ge(consts_made, 2)
            for m, value in ((ident, 1.0), (mask, MASKED)):
                nc.gpsimd.affine_select(out=m[:, :], in_=m[:, :], compare_op=ALU.not_equal, fill=value,
                                        base=0, pattern=[[-1, N]], channel_multiplier=1)\
                    .then_inc(consts_made, 1)

            def split_x(b, p, c):
                pool.wait_ge(x_hi_made, b * CHUNKS + p * 2 + c + 1)
                nc.gpsimd.tensor_tensor(x_lo[:, c % 2, :, :], X[:, :, bass.ds((p * 2 + c) * CP, CP)],
                                        x_hi[:, c % 2, :, :].bitcast(F32), ALU.subtract)\
                    .then_inc(x_lo_made, 1)

            def scale(b, along, p, c):
                g = g_no(b, along, p, c)
                pool.wait_ge(p_in[c % 2], 16 * (b * (2 * PAIRS) + along * PAIRS + p + 1))
                f = mx[:, along, bass.ds((p * 2 + c) * ROWS, ROWS)].unsqueeze(2).to_broadcast((N, ROWS, N))
                nc.gpsimd.tensor_tensor(Pe[:, c % 2, :, :], Pe[:, c % 2, :, :], f, ALU.mult)\
                    .then_inc(p_scaled, 1)

            with pool.Fori(0, B) as b:
                with pool.Fori(0, PAIRS) as p:
                    for c in range(2):
                        split_x(b, p, c)
                pool.wait_ge(f_made, (b + 1) * 2)
                scale(b, 0, 0, 0)
                nc.gpsimd.memset(V[N:P, :, :, :], 0.0).then_inc(pads_made, 1)
                scale(b, 0, 0, 1)
                for along in range(2):
                    with pool.Fori(1 - along, PAIRS) as p:
                        for c in range(2):
                            scale(b, along, p, c)

        @block.scalar
        def _(act):
            act.sem_inc(kq_evicted, 2)
            act.sem_inc(pt_made, 1)
            act.wait_ge(consts_in, 64)
            nc.scalar.activation(Wv_hi[:, :, :], X[:, 0, 0:CT * C].rearrange("p (t n) -> p t n", t=CT),
                                 ACT.Copy).then_inc(w_hi_made, 1)
            nc.scalar.activation(Wqk_hi[:, :, :], X[:, 1, 0:CT * P].rearrange("p (t n) -> p t n", t=CT),
                                 ACT.Copy).then_inc(w_hi_made, 1)

            def round_x(b, p, c):
                j, n = c % 2, p + c // 2
                act.wait_ge(x_in[j], 16 * (b * PAIRS + n + 1))
                act.wait_ge(kq_summed, b * CHUNKS + p * 2 + c + 1)
                nc.scalar.activation(x_hi[:, j, :, :], X[:, :, bass.ds((p * 2 + c) * CP, CP)], ACT.Copy)\
                    .then_inc(x_hi_made, 1)

            def evict_kq(b, p, c, v):
                u = 2 * c + v
                act.wait_ge(kq_summed, b * CHUNKS + p * 2 + c + 1 + 2)
                act.wait_ge(e_summed, e_no(b, 0, p, u))
                act.wait_ge(kq_stored, 16 * (b * SUBS + p * 4 + u))
                for i in range(2):
                    rows = slice(i * CQ, (i + 1) * CQ)
                    last = nc.scalar.activation(kq[0:CQ, i, :], kq_ps[c % 2][rows, v * SP_:(v + 1) * SP_],
                                                ACT.Identity, bias=bqk_sb[rows, :])
                last.then_inc(kq_evicted, 1)

            def exponentials(b, down, p, c):
                act.wait_ge(e_shifted, e_no(b, down, p, c) + 1 + 2)
                nc.scalar.activation(E[:, c % ERING, :, :], E[:, c % ERING, :, :], ACT.Exp)\
                    .then_inc(e_exped, 1)

            def gather_q(b, p, c):
                e = e_no(b, 1, p, c)
                act.wait_ge(e_summed, e if c == 0 else e - 1)
                src = KQ[CQ:2 * CQ, :].rearrange("p (h w) -> p w h", w=N)[:, bass.ds((p * 4 + c) * SUB, SUB), :]
                nc.scalar.activation(kq[0:CQ, c % 2, :].rearrange("p (w h) -> p w h", w=SUB), src, ACT.Copy)\
                    .then_inc(q_gathered, 1)

            def copy_turned(b, along, p, c):
                g = g_no(b, along, p, c)
                act.wait_ge(p_turned, g + 1 + 1)
                act.wait_ge(o_summed, g * ROWS)
                nc.scalar.activation(Pt[0:N, c % 2, :, :],
                                     t_ps[c % 2][0:N, 0:CP].rearrange("p (r n) -> p r n", r=ROWS), ACT.Copy)\
                    .then_inc(pt_made, 1)

            with act.Fori(0, B) as b:
                act.wait_ge(o_summed, b * (2 * CHUNKS * ROWS) + ROWS)
                round_x(b, 0, 0)
                round_x(b, 0, 1)

                def step(p, c, more):
                    evict_kq(b, p, c - 1, 0)
                    if more:
                        round_x(b, p, c + 1)
                    exponentials(b, 0, p, 2 * (c - 1))
                    evict_kq(b, p, c - 1, 1)
                    exponentials(b, 0, p, 2 * (c - 1) + 1)

                with act.Fori(0, PAIRS - 1) as p:
                    for c in (1, 2):
                        step(p, c, True)
                for c in (1, 2):
                    step(PAIRS - 1, c, False)

                act.wait_ge(kq_in, 16 * (b + 1))
                for c in range(4):
                    gather_q(b, 0, c)
                    if c:
                        exponentials(b, 1, 0, c - 1)
                with act.Fori(0, SUBS // 4 - 1) as p:
                    for c in range(4, 8):
                        gather_q(b, p, c)
                        exponentials(b, 1, p, c - 1)
                exponentials(b, 1, SUBS // 4 - 1, 3)

                act.wait_ge(st_step, b * 6 + 3)
                nc.scalar.activation(st[:, 1:3, :], st[:, 1:3, :], ACT.Exp).then_inc(st_exped, 1)

                for along in range(2):
                    with act.Fori(0, PAIRS) as p:
                        for c in range(2):
                            copy_turned(b, along, p, c)

        @block.vector
        def _(dve):
            dve.sem_inc(v_evicted, 2)
            dve.sem_inc(e_shifted, 2)
            dve.sem_inc(o_added, 2)
            nc.vector.memset(kq[CQ:P, :, :], 0.0).then_inc(kq_padded, 1)
            for hi, lo, slot, n in ((Wv_hi, Wv_lo, 0, CT * C), (Wqk_hi, Wqk_lo, 1, CT * P)):
                dve.wait_ge(w_hi_made, slot + 1)
                nc.vector.tensor_tensor(lo[:, :, :], X[:, slot, 0:n].rearrange("p (t n) -> p t n", t=CT),
                                        hi[:, :, :].bitcast(F32), ALU.subtract).then_inc(w_lo_made, 1)

            def evict_v(b, p, c, s):
                t = TILES * c + s
                dve.wait_ge(v_summed, b * (TILES * CHUNKS) + p * (2 * TILES) + t + 1)
                dve.wait_ge(v_stored[t % 2], 16 * (b * (TILES * CHUNKS // 2) + p * TILES + t // 2))
                nc.vector.tensor_tensor(v_out[:, t % 2, :], v_ps[t % 2][:, :], bv_row[:, :], ALU.add)\
                    .then_inc(v_evicted, 1)

            def shift(b, down, p, c):
                e = e_no(b, down, p, c)
                at = bass.ds((p * 4 + c) * SUB, SUB)
                ps = e_ps[c % 2][0:N, 0:SP_].rearrange("p (r n) -> p r n", r=SUB)
                m = mx[:, 1 - down, at]
                dve.wait_ge(e_summed, e + 1)
                nc.vector.tensor_reduce(m, ps, AX_X, ALU.max).then_inc(e_maxed, 1)
                dve.wait_ge(e_stored[c % ERING], 16 * (b * (2 * SUBS // ERING) + down * (SUBS // ERING) + p + c // ERING))
                dve.wait_ge(e_maxed, e + 1)
                nc.vector.tensor_tensor(E[:, c % ERING, :, :], ps, m.unsqueeze(2).to_broadcast((N, SUB, N)),
                                        ALU.subtract).then_inc(e_shifted, 1)

            def sum_z(b, down, p, c):
                dve.wait_ge(e_exped, e_no(b, down, p, c) + 1)
                nc.vector.tensor_reduce(zs[:, 1 - down, bass.ds((p * 4 + c) * SUB, SUB)], E[:, c % ERING, :, :],
                                        AX_X, ALU.add).then_inc(z_summed, 1)

            def add_attention(b, along, p, c):
                for r in range(ROWS):
                    n = g_no(b, along, p, c) * ROWS + r
                    dve.wait_ge(o_summed, n + 1 + ROWS)
                    at = (p * 2 + c) * ROWS + r
                    if along:
                        xs = X[:, :, bass.ds(at * N, N)]
                    else:
                        xs = X[:, :, :].rearrange("p t (h w) -> p t h w", w=N)[:, :, :, at]
                    nc.vector.tensor_tensor(xs, o_ps[r % 2][:, 0:CT * N].rearrange("p (t n) -> p t n", t=CT), xs,
                                            ALU.add).then_inc(o_added, 1)

            with dve.Fori(0, B) as b:
                dve.wait_ge(bv_in, 16 * (b + 1))
                for s in range(TILES):
                    evict_v(b, 0, 0, s)

                def step(p, c):
                    evict_v(b, p, c, 0)
                    evict_v(b, p, c, 1)
                    shift(b, 0, p, 2 * (c - 1))
                    sum_z(b, 0, p, 2 * (c - 1))
                    evict_v(b, p, c, 2)
                    shift(b, 0, p, 2 * (c - 1) + 1)
                    sum_z(b, 0, p, 2 * (c - 1) + 1)

                with dve.Fori(0, PAIRS - 1) as p:
                    for c in (1, 2):
                        step(p, c)
                step(PAIRS - 1, 1)
                for v in range(2):
                    shift(b, 0, PAIRS - 1, 2 + v)
                    sum_z(b, 0, PAIRS - 1, 2 + v)

                for c in range(4):
                    shift(b, 1, 0, c)
                    if c:
                        sum_z(b, 1, 0, c - 1)
                with dve.Fori(0, SUBS // 4 - 1) as p:
                    for c in range(4, 8):
                        shift(b, 1, p, c)
                        sum_z(b, 1, p, c - 1)
                sum_z(b, 1, SUBS // 4 - 1, 3)

                turned = t_ps[0][0:N, 0:2 * N].rearrange("p (k n) -> p k n", k=2)
                steps = b * 6
                dve.wait_ge(st_turned, b + 1)
                dve.wait_ge(z_summed, (b + 1) * (2 * SUBS))
                nc.vector.tensor_tensor(st[:, 0, :], turned[:, 0, :], mx[:, 0, :], ALU.max).then_inc(st_step, 1)
                dve.wait_ge(st_step, steps + 1)
                nc.vector.tensor_tensor(st[:, 1, :], mx[:, 0, :], st[:, 0, :], ALU.subtract).then_inc(st_step, 1)
                nc.vector.tensor_tensor(st[:, 2, :], turned[:, 0, :], st[:, 0, :], ALU.subtract).then_inc(st_step, 1)
                dve.wait_ge(st_exped, b + 1)
                nc.vector.tensor_tensor(st[:, 0, :], st[:, 1, :], zs[:, 0, :], ALU.mult).then_inc(st_step, 1)
                nc.vector.tensor_tensor(st[:, 3, :], turned[:, 1, :], st[:, 2, :], ALU.mult).then_inc(st_step, 1)
                dve.wait_ge(st_step, steps + 5)
                nc.vector.tensor_tensor(st[:, 0, :], st[:, 0, :], st[:, 3, :], ALU.add).then_inc(st_step, 1)
                dve.wait_ge(st_step, steps + 6)
                nc.vector.reciprocal(st[:, 3, :], st[:, 0, :]).then_inc(f_turned, 1)
                dve.wait_ge(f_turned, b * 4 + 1)
                nc.vector.tensor_scalar(st[:, 0, :], st[:, 3, :], gamma_sb[0:N, 0:1], None, ALU.mult)\
                    .then_inc(f_turned, 1)
                dve.wait_ge(f_turned, b * 4 + 2)
                nc.vector.tensor_tensor(st[:, 3, :], st[:, 2, :], st[:, 0, :], ALU.mult).then_inc(f_turned, 1)
                nc.vector.tensor_tensor(mx[:, 0, :], st[:, 1, :], st[:, 0, :], ALU.mult).then_inc(f_made, 1)
                dve.wait_ge(f_turned, b * 4 + 4)
                nc.vector.tensor_copy(mx[:, 1, :], t_ps[1][0:N, 0:N]).then_inc(f_made, 1)
                nc.vector.memset(Pt[N:P, :, :, :], 0.0).then_inc(pads_made, 1)

                for along in range(2):
                    if along:
                        dve.wait_ge(o_added, (b * (2 * CHUNKS) + CHUNKS) * ROWS + 2)
                        add_attention(b, 1, 0, 0)
                        add_attention(b, 1, 0, 1)
                    with dve.Fori(along, PAIRS) as p:
                        for c in range(2):
                            add_attention(b, along, p, c)

        @block.tensor
        def _(pe):
            pe.sem_inc(kq_summed, 2)
            pe.sem_inc(p_turned, 1)
            pe.sem_inc(o_summed, ROWS)
            pe.wait_ge(consts_made, 4)
            pe.wait_ge(kq_padded, 1)
            pe.wait_ge(w_hi_made, 2)
            pe.wait_ge(w_lo_made, 2)

            def project_v(b, p, c, s):
                j, t = c % 2, TILES * c + s
                if s == 0:
                    pe.wait_ge(x_hi_made, b * CHUNKS + p * 2 + c + 1)
                    pe.wait_ge(x_lo_made, b * CHUNKS + p * 2 + c + 1)
                pe.wait_ge(v_evicted, b * (TILES * CHUNKS) + p * (2 * TILES) + t + 1)
                at = slice(s * P, (s + 1) * P)
                for ct in range(CT):
                    for a, w in ((x_hi, Wv_hi), (x_hi, Wv_lo), (x_lo, Wv_hi)):
                        last = nc.tensor.matmul(v_ps[t % 2][:, :], a[:, j, ct, at], w[:, ct, :],
                                                start=(ct == 0 and w is Wv_hi and a is x_hi),
                                                stop=(ct == CT - 1 and a is x_lo))
                last.then_inc(v_summed, 1)

            def project_kq(b, p, c):
                j = c % 2
                pe.wait_ge(kq_evicted, b * SUBS + p * 4 + 2 * c)
                for ct in range(CT):
                    for w, a in ((Wqk_hi, x_hi), (Wqk_hi, x_lo), (Wqk_lo, x_hi)):
                        last = nc.tensor.matmul(kq_ps[j][:, 0:CP], w[:, ct, :], a[:, j, ct, :],
                                                start=(ct == 0 and w is Wqk_hi and a is x_hi),
                                                stop=(ct == CT - 1 and w is Wqk_lo))
                last.then_inc(kq_summed, 1)

            def row_energies(b, p, c):
                e = e_no(b, 0, p, c)
                pe.wait_ge(kq_evicted, b * SUBS + p * 4 + c + 1 + 2)
                pe.wait_ge(e_shifted, e + 1)
                for r in range(SUB):
                    at = slice(r * N, (r + 1) * N)
                    last = nc.tensor.matmul(e_ps[c % 2][0:N, at], kq[:, 1, at], kq[:, 0, at], start=True, stop=True)
                last.then_inc(e_summed, 1)

            def column_energies(b, p, c):
                e = e_no(b, 1, p, c)
                pe.wait_ge(q_gathered, b * SUBS + p * 4 + c + 1)
                pe.wait_ge(e_shifted, e + 1)
                for r in range(SUB):
                    out_ = e_ps[c % 2][0:N, r * N:(r + 1) * N]
                    k = KQ[:, :].rearrange("p (h w) -> p h w", w=N)[:, :, (p * 4 + c) * SUB + r]
                    nc.tensor.matmul(out_, ident[:, :], mask[:, :], start=True, stop=False)
                    last = nc.tensor.matmul(out_, kq[:, c % 2, r * N:(r + 1) * N], k, start=False, stop=True)
                last.then_inc(e_summed, 1)

            def turn(b, along, p, c):
                g = g_no(b, along, p, c)
                pe.wait_ge(p_scaled, g + 1)
                pe.wait_ge(pt_made, g)
                for r in range(ROWS):
                    last = nc.tensor.transpose(t_ps[c % 2][0:N, r * N:(r + 1) * N], Pe[:, c % 2, r, :], ident[:, :])
                last.then_inc(p_turned, 1)

            def attend(b, along, p, c):
                g = g_no(b, along, p, c)
                j = c % 2
                pe.wait_ge(pt_made, g + 1 + 1)
                pe.wait_ge(v_in[j], 16 * (b * (2 * PAIRS) + along * PAIRS + p + c // 2 + 1))
                for r in range(ROWS):
                    pe.wait_ge(o_added, g * ROWS + r + 1)
                    for ct in range(CT):
                        last = nc.tensor.matmul(o_ps[r % 2][:, ct * N:(ct + 1) * N],
                                                V[:, j, r, ct * P:(ct + 1) * P], Pt[:, j, r, :],
                                                start=True, stop=True)
                    last.then_inc(o_summed, 1)

            with pe.Fori(0, B) as b:
                def step(p, c):
                    project_v(b, p, c, 0)
                    project_v(b, p, c, 1)
                    row_energies(b, p, 2 * (c - 1))
                    project_v(b, p, c, 2)
                    row_energies(b, p, 2 * (c - 1) + 1)
                    project_kq(b, p, c)

                for s in range(TILES):
                    project_v(b, 0, 0, s)
                project_kq(b, 0, 0)
                with pe.Fori(0, PAIRS - 1) as p:
                    for c in (1, 2):
                        step(p, c)
                step(PAIRS - 1, 1)
                for v in range(2):
                    row_energies(b, PAIRS - 1, 2 + v)

                with pe.Fori(0, SUBS // 4) as p:
                    for c in range(4):
                        column_energies(b, p, c)

                pe.wait_ge(z_summed, (b + 1) * (2 * SUBS))
                nc.tensor.transpose(t_ps[0][0:N, 0:N], mx[:, 1, :], ident[:, :])
                nc.tensor.transpose(t_ps[0][0:N, N:2 * N], zs[:, 1, :], ident[:, :]).then_inc(st_turned, 1)
                pe.wait_ge(f_turned, b * 4 + 3)
                nc.tensor.transpose(t_ps[1][0:N, 0:N], st[:, 3, :], ident[:, :]).then_inc(f_turned, 1)

                pe.wait_ge(pads_made, (b + 1) * 2)
                for along in range(2):
                    turn(b, along, 0, 0)
                    with pe.Fori(0, PAIRS - 1) as p:
                        for c in range(2):
                            turn(b, along, p, c + 1)
                            attend(b, along, p, c)
                    turn(b, along, PAIRS - 1, 1)
                    attend(b, along, PAIRS - 1, 0)
                    attend(b, along, PAIRS - 1, 1)


def kernel(**inputs):
    import numpy as np
    import concourse.bacc as bacc
    from concourse.bass_utils import run_bass_kernel_spmd

    w = {k: np.asarray(v) for k, v in inputs.items()}
    arrays = {
        "x": w["x"],
        "wqk_t": np.ascontiguousarray(np.concatenate([w["L0_conv_Wk"], w["L0_conv_Wq"]], 0).T),
        "wv_t": np.ascontiguousarray(w["L0_conv_Wv"].T),
        "bqk": np.concatenate([w["L0_conv_bk"], w["L0_conv_bq"]])[:, None],
        "bv": w["L0_conv_bv"][None, :],
        "gamma": w["L0_conv_gamma"][None, :],
    }
    nc = bacc.Bacc("TRN2", target_bir_lowering=False, num_devices=1)
    args = [nc.dram_tensor(f"in_{k}", a.shape, F32, kind="ExternalInput").ap() for k, a in arrays.items()]
    out = nc.dram_tensor("out", w["x"].shape, F32, kind="ExternalOutput").ap()
    criss_cross_attention(nc, *args, out)
    r = run_bass_kernel_spmd(nc, [{f"in_{k}": a for k, a in arrays.items()}], core_ids=[0])
    return r.results[0]["out"]
```

```python
from contextlib import ExitStack

import concourse.bass as bass
from concourse import mybir

ALU = mybir.AluOpType
ACT = mybir.ActivationFunctionType
AX_X = mybir.AxisListType.X
F32 = mybir.dt.float32
F32R = mybir.dt.float32r

P = 128
N = 96
POS = N * N
ROWS = 4
CP = ROWS * N
CHUNKS = N // ROWS
PAIRS = CHUNKS // 2
TILES = CP // P
SUB = 2
SP_ = SUB * N
SUBS = N // SUB
ERING = 4
GROUP = 4
GROUPS = N // GROUP
RING = 3
TRIPLES = CHUNKS // RING
WIDE = 128


def criss_cross_attention(nc, x, wqk_t, wv_t, bqk, bv, gamma, out):
    B, C = x.shape[0], x.shape[1]
    CT = C // P
    CQ = wqk_t.shape[1] // 2
    assert x.shape[2] == N and x.shape[3] == N and C % P == 0 and 2 * CQ == P and CP % P == 0

    v_dram = nc.dram_tensor("v_scratch", (B, POS, C), F32, kind="Internal").ap()
    kq_dram = nc.dram_tensor("kq_scratch", (B, 2, CQ, POS), F32, kind="Internal").ap()
    e_dram = nc.dram_tensor("e_scratch", (2, B, N, N, N), F32, kind="Internal").ap()

    x_v = x.rearrange("b (t p) h w -> b p t (h w)", p=P)
    out_v = out.rearrange("b (t p) h w -> b p t (h w)", p=P)
    v_by_column = v_dram.rearrange("b (g w) c -> b g w c", g=N)
    v_by_row = v_dram.rearrange("b (h u) c -> b u h c", h=N)

    ctx = ExitStack()
    with ctx:
        def sb(name, shape, dt=F32, at=None):
            return (at or ctx).enter_context(nc.sbuf_tensor(name, shape, dt))

        def sem(name):
            return ctx.enter_context(nc.semaphore(name))

        X = sb("X", [P, CT, POS])
        Wv_hi = sb("Wv_hi", [P, CT, C], F32R)
        Wv_lo = sb("Wv_lo", [P, CT, C], F32R)
        Wqk_hi = sb("Wqk_hi", [P, CT, P], F32R)
        Wqk_lo = sb("Wqk_lo", [P, CT, P], F32R)
        bqk_sb = sb("bqk_sb", [P, 1])
        gamma_sb = sb("gamma_sb", [P, 1])
        kq = sb("kq", [P, 2, SP_])
        E = sb("E", [N, RING * GROUP, N])
        E_rows = E[:, 0:ERING * SUB, :].rearrange("p (e r) n -> p e r n", r=SUB)
        E_cols = E[:, :, :].rearrange("p (e r) n -> p e r n", r=GROUP)
        mx = sb("mx", [N, 2, N])
        zs = sb("zs", [N, 2, N])
        with ExitStack() as s1:
            x_split = sb("x_split", [P, 2, 2, CT, CP], F32R, s1)
            gap = sb("gap", [P, POS - 4 * CT * CP - (TILES + 1) * C], F32, s1)
            v_out = sb("v_out", [P, TILES, C], F32, s1)
            bv_row = sb("bv_row", [P, C], F32, s1)
        with ExitStack() as s2:
            KQ = sb("KQ", [P, POS], F32, s2)
        with ExitStack() as s3:
            V = sb("V", [P, RING, ROWS, C], F32, s3)
            Pe = sb("Pe", [N, RING, ROWS, N], F32, s3)
            Pt = sb("Pt", [P, RING, CP + WIDE - N], F32, s3)
            st = sb("st", [N, 4, N], F32, s3)
            ident = sb("ident", [N, N], F32, s3)
        slot_rows = 2 * CT * CP // N
        gap_rows = (gap.shape[1]) // N

        bank = [ctx.enter_context(nc.psum_tensor(f"bank{i}", [P, 512], F32)) for i in range(8)]
        v_ps, kq_ps, e_ps = bank[0:2], bank[2:4], bank[4:6]
        ce_ps = bank[5:8]
        t_ps, o_ps = bank[2:5], bank[6:8] + bank[0:2]

        consts_in = sem("consts_in")
        kq_padded = sem("kq_padded")
        w_hi_made = sem("w_hi_made")
        w_lo_made = sem("w_lo_made")
        x_in = [sem(f"x_in{j}") for j in range(2)]
        bv_in = sem("bv_in")
        x_hi_made = sem("x_hi_made")
        x_lo_made = sem("x_lo_made")
        v_summed = sem("v_summed")
        v_evicted = sem("v_evicted")
        v_stored = [sem(f"v_stored{j}") for j in range(TILES)]
        kq_summed = sem("kq_summed")
        kq_evicted = sem("kq_evicted")
        kq_stored = sem("kq_stored")
        sync_stages = sem("sync_stages")
        kq_in = sem("kq_in")
        e_summed = sem("e_summed")
        e_maxed = sem("e_maxed")
        e_shifted = sem("e_shifted")
        e_exped = sem("e_exped")
        e_stored = [sem(f"e_stored{j}") for j in range(ERING)]
        q_gathered = sem("q_gathered")
        c_summed = sem("c_summed")
        c_maxed = sem("c_maxed")
        c_shifted = sem("c_shifted")
        c_exped = sem("c_exped")
        c_masking = sem("c_masking")
        c_masked = sem("c_masked")
        c_stored = [sem(f"c_stored{j}") for j in range(RING)]
        z_summed = sem("z_summed")
        ident_made = sem("ident_made")
        st_turned = sem("st_turned")
        st_step = sem("st_step")
        st_exped = sem("st_exped")
        f_turned = sem("f_turned")
        f_made = sem("f_made")
        v_in = [sem(f"v_in{j}") for j in range(RING)]
        p_in = [sem(f"p_in{j}") for j in range(RING)]
        pads_made = sem("pads_made")
        p_scaled = sem("p_scaled")
        p_turned = sem("p_turned")
        pt_made = sem("pt_made")
        o_summed = sem("o_summed")
        o_added = sem("o_added")
        out_stored = [sem(f"out_stored{j}") for j in range(2)]

        def g_no(b, along, p, c):
            return b * (2 * CHUNKS) + CHUNKS * along + p * RING + c

        START = {x_in[0]: 16, x_in[1]: 16, kq_stored: 16, **{s: 16 for s in v_stored + e_stored + c_stored},
                 out_stored[0]: 16 * PAIRS, out_stored[1]: 16 * PAIRS,
                 kq_evicted: 3, v_evicted: 2, v_summed: TILES + 1, e_shifted: 2, c_shifted: 3, e_summed: 1,
                 c_summed: 2, pt_made: 3, p_turned: 3, o_summed: 2 * ROWS + 1, o_added: 4}

        def past(s, n):
            return n + START[s]

        block = ctx.enter_context(nc.Block())

        @block.sync
        def _(sp):
            for s in (*x_in, *v_stored, kq_stored, *e_stored, *c_stored, *out_stored):
                sp.sem_inc(s, START[s])
            sp.dma_start(X[:, 0, 0:CT * C].rearrange("p (t n) -> p t n", t=CT),
                         wv_t.rearrange("(t p) n -> p t n", p=P)).then_inc(consts_in, 16)
            sp.dma_start(X[:, 1, 0:CT * P].rearrange("p (t n) -> p t n", t=CT),
                         wqk_t.rearrange("(t p) n -> p t n", p=P)).then_inc(consts_in, 16)
            sp.dma_start(bqk_sb[:, :], bqk).then_inc(consts_in, 16)
            sp.dma_start(gamma_sb[:, :], gamma.to_broadcast((P, 1))).then_inc(consts_in, 16)
            sp.wait_ge(w_hi_made, 2)
            sp.wait_ge(w_lo_made, 2)

            def load_x(b, p, c):
                j, n = c % 2, p + c // 2
                sp.wait_ge(x_in[j], past(x_in[j], 16 * (b * PAIRS + n)))
                sp.wait_ge(out_stored[j], past(out_stored[j], 16 * ((b - 1) * PAIRS + n + 1)))
                at = bass.ds((p * 2 + c) * CP, CP)
                sp.dma_start(X[:, :, at], x_v[b, :, :, at]).then_inc(x_in[j], 16)

            def store_v(b, p, c, s):
                sp.wait_ge(v_evicted, past(v_evicted, b * (TILES * CHUNKS) + p * (2 * TILES) + TILES * c + s + 1))
                sp.dma_start(v_dram[b, bass.ds(p * (2 * CP) + (TILES * c + s) * P, P), :], v_out[:, s, :])\
                    .then_inc(v_stored[s], 16)

            def store_kq(b, p, c, v):
                u = 2 * c + v
                sp.wait_ge(kq_evicted, past(kq_evicted, b * SUBS + p * 4 + u + 1))
                sp.dma_start(kq_dram[b, :, :, bass.ds((p * 4 + u) * SP_, SP_)].rearrange("t c n -> c t n"),
                             kq[0:CQ, :, :]).then_inc(kq_stored, 16)

            def store_e(b, p, c, v):
                u = 2 * c + v
                sp.wait_ge(e_exped, b * SUBS + p * 4 + u + 1)
                sp.dma_start(e_dram[1, b, :, bass.ds((p * 4 + u) * SUB, SUB), :], E_rows[:, u % ERING, :, :])\
                    .then_inc(e_stored[u % ERING], 16)

            def load_kq(b, first_row, rows):
                at = slice(first_row * N, (first_row + rows) * N)
                sp.dma_start(KQ[:, at], kq_dram[b, :, :, at].rearrange("t c n -> (t c) n")).then_inc(kq_in, 16)

            def store_c(b, p, c):
                sp.wait_ge(c_masked, b * GROUPS + p * RING + c + 1)
                sp.dma_start(e_dram[0, b, :, bass.ds((p * RING + c) * GROUP, GROUP), :], E_cols[:, c, :, :])\
                    .then_inc(c_stored[c], 16)

            def load_attention(b, along, p, c):
                g = g_no(b, along, p, c)
                at = bass.ds((p * RING + c) * ROWS, ROWS)
                sp.wait_ge(p_turned, past(p_turned, g - 2))
                sp.dma_start(Pe[:, c, :, :], e_dram[along, b, :, at, :]).then_inc(p_in[c], 16)
                sp.wait_ge(o_summed, past(o_summed, (g - 2) * ROWS))
                sp.dma_start(V[0:N, c, :, :], (v_by_row if along else v_by_column)[b, :, at, :])\
                    .then_inc(v_in[c], 16)

            def store_out(b, p, c):
                sp.wait_ge(o_added, past(o_added, (b * (2 * CHUNKS) + CHUNKS + p * 2 + c + 1) * ROWS))
                at = bass.ds((p * 2 + c) * CP, CP)
                sp.dma_start(out_v[b, :, :, at], X[:, :, at]).then_inc(out_stored[c % 2], 16)

            def next_x(b, p, c, drains):
                load_x(b, p, c)
                if drains:
                    store_out(b - 1, p, c + 2)

            def first_stage(b, drains):
                next_x(b, 0, 2, drains)
                sp.wait_ge(o_summed, past(o_summed, b * (2 * CHUNKS * ROWS)))
                sp.dma_start(bv_row[:, :], bv.to_broadcast((P, C))).then_inc(bv_in, 16)

                def stores(p, c, part_of_kq=False):
                    store_kq(b, p, c, 0)
                    store_v(b, p, c, 0)
                    if part_of_kq:
                        load_kq(b, 2 * slot_rows, gap_rows)
                    store_v(b, p, c, 1)
                    store_kq(b, p, c, 1)
                    store_e(b, p, c, 0)
                    store_v(b, p, c, 2)
                    store_e(b, p, c, 1)

                with sp.Fori(0, PAIRS - 3) as p:
                    for c in range(2):
                        next_x(b, p, c + 3, drains)
                        stores(p, c)
                for c in range(5):
                    if c < 3:
                        next_x(b, PAIRS - 3, c + 3, drains and c == 0)
                    stores(PAIRS - 3, c)
                sp.wait_ge(v_summed, past(v_summed, (b + 1) * (TILES * CHUNKS) - TILES))
                sp.sem_inc(sync_stages, 1)
                load_kq(b, 0, slot_rows)
                stores(PAIRS - 1, 1, part_of_kq=True)

            def other_stages(b, last):
                sp.wait_ge(v_summed, past(v_summed, (b + 1) * (TILES * CHUNKS)))
                load_kq(b, slot_rows, slot_rows)
                for s in range(TILES):
                    sp.wait_ge(v_stored[s], past(v_stored[s], (b + 1) * (16 * CHUNKS)))
                sp.sem_inc(sync_stages, 1)
                sp.wait_ge(kq_stored, past(kq_stored, (b + 1) * (16 * SUBS)))
                load_kq(b, 2 * slot_rows + gap_rows, N - 2 * slot_rows - gap_rows)
                with sp.Fori(0, TRIPLES) as p:
                    for c in range(RING):
                        store_c(b, p, c)
                for j in range(ERING):
                    sp.wait_ge(e_stored[j], past(e_stored[j], (b + 1) * (16 * SUBS // ERING)))
                sp.sem_inc(sync_stages, 1)
                for j in range(RING):
                    sp.wait_ge(c_stored[j], past(c_stored[j], (b + 1) * (16 * TRIPLES)))
                sp.sem_inc(sync_stages, 1)
                for c in range(RING):
                    load_attention(b, 0, 0, c)
                with sp.Fori(1, TRIPLES) as p:
                    for c in range(RING):
                        load_attention(b, 0, p, c)
                if last:
                    for c in range(RING):
                        load_attention(b, 1, 0, c)
                    with sp.Fori(0, CHUNKS // (2 * RING) - 1) as p:
                        for c in range(2 * RING):
                            load_attention(b, 1, p * 2 + 1 + c // RING, c % RING)
                            store_out(b, p * RING, c)
                    for c in range(RING):
                        load_attention(b, 1, TRIPLES - 1, c)
                        store_out(b, PAIRS - RING, c)
                    for c in range(RING):
                        store_out(b, PAIRS - RING, RING + c)
                else:
                    with sp.Fori(0, TRIPLES - 1) as p:
                        for c in range(RING):
                            load_attention(b, 1, p, c)
                    for c in range(RING):
                        load_attention(b, 1, TRIPLES - 1, c)
                        if c:
                            store_out(b, 0, c - 1)
                    for c in range(2):
                        next_x(b + 1, 0, c, True)

            for c in range(2):
                load_x(0, 0, c)
            first_stage(0, False)
            with sp.Fori(0, B - 1) as b:
                other_stages(b, False)
                first_stage(b + 1, True)
            other_stages(B - 1, True)
            for j in range(2):
                sp.wait_ge(out_stored[j], past(out_stored[j], 16 * PAIRS * B))

        @block.gpsimd
        def _(pool):
            def split_x(b, p, c):
                pool.wait_ge(x_hi_made, b * CHUNKS + p * 2 + c + 1)
                nc.gpsimd.tensor_tensor(x_split[:, c % 2, 1, :, :], X[:, :, bass.ds((p * 2 + c) * CP, CP)],
                                        x_split[:, c % 2, 0, :, :].bitcast(F32), ALU.subtract)\
                    .then_inc(x_lo_made, 1)

            def mask(b, p, c):
                pool.wait_ge(c_exped, b * GROUPS + p * RING + c + 1)
                pool.sem_inc(c_masking, 1)
                nc.gpsimd.affine_select(out=E_cols[:, c, :, :], in_=E_cols[:, c, :, :], compare_op=ALU.not_equal,
                                        fill=0.0, base=0, pattern=[[0, GROUP], [-1, N]], channel_multiplier=1)\
                    .then_inc(c_masked, 1)

            def scale(b, along, p, c):
                pool.wait_ge(p_in[c], 16 * (b * (2 * TRIPLES) + along * TRIPLES + p + 1))
                f = mx[:, along, bass.ds((p * RING + c) * ROWS, ROWS)].unsqueeze(2).to_broadcast((N, ROWS, N))
                nc.gpsimd.tensor_tensor(Pe[:, c, :, :], Pe[:, c, :, :], f, ALU.mult)\
                    .then_inc(p_scaled, 1)

            with pool.Fori(0, B) as b:
                with pool.Fori(0, PAIRS) as p:
                    for c in range(2):
                        split_x(b, p, c)
                with pool.Fori(0, TRIPLES) as p:
                    for c in range(RING):
                        mask(b, p, c)
                pool.wait_ge(c_summed, past(c_summed, (b + 1) * (2 * GROUPS)))
                pool.sem_inc(c_masking, 1)
                nc.gpsimd.memset(ident[:, :], 0.0).then_inc(ident_made, 1)
                pool.wait_ge(ident_made, b * 2 + 1)
                pool.sem_inc(c_masking, 1)
                nc.gpsimd.affine_select(out=ident[:, :], in_=ident[:, :], compare_op=ALU.not_equal, fill=1.0,
                                        base=0, pattern=[[-1, N]], channel_multiplier=1).then_inc(ident_made, 1)
                nc.gpsimd.memset(V[N:P, 0, :, :], 0.0).then_inc(pads_made, 1)
                pool.wait_ge(f_made, (b + 1) * 2)
                scale(b, 0, 0, 0)
                nc.gpsimd.memset(V[N:P, 1, :, :], 0.0).then_inc(pads_made, 1)
                scale(b, 0, 0, 1)
                nc.gpsimd.memset(V[N:P, 2, :, :], 0.0).then_inc(pads_made, 1)
                scale(b, 0, 0, 2)
                for along in range(2):
                    with pool.Fori(1 - along, TRIPLES) as p:
                        for c in range(RING):
                            scale(b, along, p, c)

        @block.scalar
        def _(act):
            act.sem_inc(kq_evicted, START[kq_evicted])
            act.sem_inc(pt_made, START[pt_made])
            act.wait_ge(consts_in, 64)
            nc.scalar.activation(Wv_hi[:, :, :], X[:, 0, 0:CT * C].rearrange("p (t n) -> p t n", t=CT),
                                 ACT.Copy).then_inc(w_hi_made, 1)
            nc.scalar.activation(Wqk_hi[:, :, :], X[:, 1, 0:CT * P].rearrange("p (t n) -> p t n", t=CT),
                                 ACT.Copy).then_inc(w_hi_made, 1)

            def round_x(b, p, c):
                j, n = c % 2, p + c // 2
                act.wait_ge(x_in[j], past(x_in[j], 16 * (b * PAIRS + n + 1)))
                act.wait_ge(v_summed, past(v_summed, (b * CHUNKS + p * 2 + c - 1) * TILES))
                nc.scalar.activation(x_split[:, j, 0, :, :], X[:, :, bass.ds((p * 2 + c) * CP, CP)], ACT.Copy)\
                    .then_inc(x_hi_made, 1)

            def evict_kq(b, p, c, v):
                u = 2 * c + v
                act.wait_ge(kq_summed, b * CHUNKS + p * 2 + c + 1)
                act.wait_ge(e_summed, past(e_summed, b * SUBS + p * 4 + u))
                act.wait_ge(kq_stored, past(kq_stored, 16 * (b * SUBS + p * 4 + u)))
                for i in range(2):
                    rows = slice(i * CQ, (i + 1) * CQ)
                    last = nc.scalar.activation(kq[0:CQ, i, :], kq_ps[c % 2][rows, v * SP_:(v + 1) * SP_],
                                                ACT.Identity, bias=bqk_sb[rows, :])
                last.then_inc(kq_evicted, 1)

            def exponentials(b, p, c):
                act.wait_ge(e_shifted, past(e_shifted, b * SUBS + p * 4 + c + 1))
                nc.scalar.activation(E_rows[:, c % ERING, :, :], E_rows[:, c % ERING, :, :], ACT.Exp)\
                    .then_inc(e_exped, 1)

            def gather_q(b, p, c, v):
                u = (p * RING + c) * 2 + v
                act.wait_ge(c_summed, past(c_summed, b * (2 * GROUPS) + u - 1))
                src = KQ[CQ:2 * CQ, :].rearrange("p (h w) -> p w h", w=N)[:, bass.ds(u * 2, 2), :]
                nc.scalar.activation(kq[0:CQ, v, :].rearrange("p (w h) -> p w h", w=2), src, ACT.Copy)\
                    .then_inc(q_gathered, 1)

            def exponentials_c(b, p, c):
                act.wait_ge(c_shifted, past(c_shifted, b * GROUPS + p * RING + c + 1))
                nc.scalar.activation(E_cols[:, c % RING, :, :], E_cols[:, c % RING, :, :], ACT.Exp)\
                    .then_inc(c_exped, 1)

            def copy_turned(b, along, p, c):
                g = g_no(b, along, p, c)
                act.wait_ge(p_turned, past(p_turned, g + 1))
                act.wait_ge(o_summed, past(o_summed, (g - 2) * ROWS))
                nc.scalar.activation(Pt[0:N, c, 0:CP], t_ps[c][0:N, 0:CP], ACT.Copy)\
                    .then_inc(pt_made, 1)

            with act.Fori(0, B) as b:
                act.wait_ge(o_summed, past(o_summed, b * (2 * CHUNKS * ROWS)))
                round_x(b, 0, 0)

                def step(p, c, more):
                    evict_kq(b, p, c, 0)
                    if more:
                        round_x(b, p, c + 1)
                    evict_kq(b, p, c, 1)
                    exponentials(b, p, 2 * c)
                    exponentials(b, p, 2 * c + 1)

                with act.Fori(0, PAIRS - 1) as p:
                    for c in range(2):
                        step(p, c, True)
                for c in range(2):
                    step(PAIRS - 1, c, c == 0)

                act.wait_ge(kq_in, 64 * (b + 1))
                for c in range(RING):
                    for v in range(2):
                        gather_q(b, 0, c, v)
                    if c == RING - 1:
                        exponentials_c(b, 0, 0)
                with act.Fori(0, TRIPLES - 1) as p:
                    for c in range(RING, 2 * RING):
                        for v in range(2):
                            gather_q(b, p, c, v)
                        exponentials_c(b, p, c - 2)
                exponentials_c(b, TRIPLES - 1, 1)
                exponentials_c(b, TRIPLES - 1, 2)

                act.wait_ge(st_step, b * 6 + 3)
                nc.scalar.activation(st[:, 1:3, :], st[:, 1:3, :], ACT.Exp).then_inc(st_exped, 1)

                for along in range(2):
                    with act.Fori(0, TRIPLES) as p:
                        for c in range(RING):
                            copy_turned(b, along, p, c)

        @block.vector
        def _(dve):
            dve.sem_inc(v_evicted, START[v_evicted])
            dve.sem_inc(e_shifted, START[e_shifted])
            dve.sem_inc(c_shifted, START[c_shifted])
            dve.sem_inc(o_added, START[o_added])
            nc.vector.memset(kq[CQ:P, :, :], 0.0).then_inc(kq_padded, 1)
            for hi, lo, slot, n in ((Wv_hi, Wv_lo, 0, CT * C), (Wqk_hi, Wqk_lo, 1, CT * P)):
                dve.wait_ge(w_hi_made, slot + 1)
                nc.vector.tensor_tensor(lo[:, :, :], X[:, slot, 0:n].rearrange("p (t n) -> p t n", t=CT),
                                        hi[:, :, :].bitcast(F32), ALU.subtract).then_inc(w_lo_made, 1)

            def evict_v(b, p, c, s):
                t = TILES * c + s
                dve.wait_ge(v_summed, past(v_summed, b * (TILES * CHUNKS) + p * (2 * TILES) + t + 1))
                dve.wait_ge(v_stored[s], past(v_stored[s], 16 * (b * CHUNKS + p * 2 + c)))
                nc.vector.tensor_tensor(v_out[:, s, :], v_ps[t % 2][:, :], bv_row[:, :], ALU.add)\
                    .then_inc(v_evicted, 1)

            def shift(b, p, c):
                e = b * SUBS + p * 4 + c
                ps = e_ps[c % 2][0:N, 0:SP_].rearrange("p (r n) -> p r n", r=SUB)
                m = mx[:, 1, bass.ds((p * 4 + c) * SUB, SUB)]
                dve.wait_ge(e_summed, past(e_summed, e + 1))
                nc.vector.tensor_reduce(m, ps, AX_X, ALU.max).then_inc(e_maxed, 1)
                dve.wait_ge(e_stored[c % ERING], past(e_stored[c % ERING], 16 * (b * (SUBS // ERING) + p + c // ERING)))
                dve.wait_ge(e_maxed, e + 1)
                nc.vector.tensor_tensor(E_rows[:, c % ERING, :, :], ps, m.unsqueeze(2).to_broadcast((N, SUB, N)),
                                        ALU.subtract).then_inc(e_shifted, 1)

            def sum_z(b, p, c):
                dve.wait_ge(e_exped, b * SUBS + p * 4 + c + 1)
                nc.vector.tensor_reduce(zs[:, 1, bass.ds((p * 4 + c) * SUB, SUB)], E_rows[:, c % ERING, :, :],
                                        AX_X, ALU.add).then_inc(z_summed, 1)

            def group_of(p, c):
                ps = ce_ps[c % RING][0:N, 0:GROUP * N].rearrange("p (r n) -> p r n", r=GROUP)
                return ps, mx[:, 0, bass.ds((p * RING + c) * GROUP, GROUP)]

            def max_c(b, p, c):
                ps, m = group_of(p, c)
                dve.wait_ge(c_summed, past(c_summed, 2 * (b * GROUPS + p * RING + c + 1)))
                nc.vector.tensor_reduce(m, ps, AX_X, ALU.max).then_inc(c_maxed, 1)

            def shift_c(b, p, c):
                ps, m = group_of(p, c)
                dve.wait_ge(c_stored[c % RING], past(c_stored[c % RING], 16 * (b * TRIPLES + p + c // RING)))
                dve.wait_ge(c_maxed, b * GROUPS + p * RING + c + 1)
                nc.vector.tensor_tensor(E_cols[:, c % RING, :, :], ps, m.unsqueeze(2).to_broadcast((N, GROUP, N)),
                                        ALU.subtract).then_inc(c_shifted, 1)

            def sum_c(b, p, c):
                dve.wait_ge(c_masked, b * GROUPS + p * RING + c + 1)
                nc.vector.tensor_reduce(zs[:, 0, bass.ds((p * RING + c) * GROUP, GROUP)], E_cols[:, c % RING, :, :],
                                        AX_X, ALU.add).then_inc(z_summed, 1)

            def add_attention(b, along, p, c):
                for r in range(ROWS):
                    n = g_no(b, along, p, c) * ROWS + r
                    dve.wait_ge(o_summed, past(o_summed, n + 1))
                    at = (p * RING + c) * ROWS + r
                    if along:
                        xs = X[:, :, bass.ds(at * N, N)]
                    else:
                        xs = X[:, :, :].rearrange("p t (h w) -> p t h w", w=N)[:, :, :, at]
                    nc.vector.tensor_tensor(xs, o_ps[r][:, :].rearrange("p (t n) -> p t n", t=CT)[:, :, 0:N], xs,
                                            ALU.add).then_inc(o_added, 1)

            with dve.Fori(0, B) as b:
                dve.wait_ge(bv_in, 16 * (b + 1))

                def step(p, c):
                    evict_v(b, p, c, 0)
                    evict_v(b, p, c, 1)
                    shift(b, p, 2 * c)
                    evict_v(b, p, c, 2)
                    sum_z(b, p, 2 * c)
                    shift(b, p, 2 * c + 1)
                    sum_z(b, p, 2 * c + 1)

                for c in range(2):
                    step(0, c)
                with dve.Fori(1, PAIRS) as p:
                    for c in range(2):
                        step(p, c)

                max_c(b, 0, 0)
                for j in range(ERING):
                    dve.wait_ge(e_stored[j], past(e_stored[j], 16 * (b + 1) * (SUBS // ERING)))
                for c in range(1, 4):
                    if c == 3:
                        sum_c(b, 0, 0)
                    max_c(b, 0, c)
                    shift_c(b, 0, c - 1)
                with dve.Fori(0, TRIPLES - 2) as p:
                    for c in range(4, 4 + RING):
                        sum_c(b, p, c - 3)
                        max_c(b, p, c)
                        shift_c(b, p, c - 1)
                for c in (4, 5):
                    sum_c(b, TRIPLES - 2, c - 3)
                    max_c(b, TRIPLES - 2, c)
                    shift_c(b, TRIPLES - 2, c - 1)
                sum_c(b, TRIPLES - 1, 0)
                shift_c(b, TRIPLES - 1, 2)
                sum_c(b, TRIPLES - 1, 1)
                sum_c(b, TRIPLES - 1, 2)

                turned = t_ps[0][0:N, 0:2 * N].rearrange("p (k n) -> p k n", k=2)
                steps = b * 6
                dve.wait_ge(st_turned, b + 1)
                dve.wait_ge(z_summed, (b + 1) * (SUBS + GROUPS))
                nc.vector.tensor_tensor(st[:, 0, :], turned[:, 0, :], mx[:, 0, :], ALU.max).then_inc(st_step, 1)
                dve.wait_ge(st_step, steps + 1)
                nc.vector.tensor_tensor(st[:, 1, :], mx[:, 0, :], st[:, 0, :], ALU.subtract).then_inc(st_step, 1)
                nc.vector.tensor_tensor(st[:, 2, :], turned[:, 0, :], st[:, 0, :], ALU.subtract).then_inc(st_step, 1)
                dve.wait_ge(st_exped, b + 1)
                nc.vector.tensor_tensor(st[:, 0, :], st[:, 1, :], zs[:, 0, :], ALU.mult).then_inc(st_step, 1)
                nc.vector.tensor_tensor(st[:, 3, :], turned[:, 1, :], st[:, 2, :], ALU.mult).then_inc(st_step, 1)
                dve.wait_ge(st_step, steps + 5)
                nc.vector.tensor_tensor(st[:, 0, :], st[:, 0, :], st[:, 3, :], ALU.add).then_inc(st_step, 1)
                dve.wait_ge(st_step, steps + 6)
                nc.vector.reciprocal(st[:, 3, :], st[:, 0, :]).then_inc(f_turned, 1)
                dve.wait_ge(f_turned, b * 4 + 1)
                nc.vector.tensor_scalar(st[:, 0, :], st[:, 3, :], gamma_sb[0:N, 0:1], None, ALU.mult)\
                    .then_inc(f_turned, 1)
                dve.wait_ge(f_turned, b * 4 + 2)
                nc.vector.tensor_tensor(st[:, 3, :], st[:, 2, :], st[:, 0, :], ALU.mult).then_inc(f_turned, 1)
                nc.vector.tensor_tensor(mx[:, 0, :], st[:, 1, :], st[:, 0, :], ALU.mult).then_inc(f_made, 1)
                dve.wait_ge(f_turned, b * 4 + 4)
                nc.vector.tensor_copy(mx[:, 1, :], t_ps[1][0:N, 0:N]).then_inc(f_made, 1)
                nc.vector.memset(Pt[N:P, :, :], 0.0).then_inc(pads_made, 1)
                nc.vector.memset(Pt[0:N, :, CP:], 0.0).then_inc(pads_made, 1)

                for along in range(2):
                    if along:
                        dve.wait_ge(o_added, past(o_added, (b * (2 * CHUNKS) + CHUNKS) * ROWS))
                        for c in range(RING):
                            add_attention(b, 1, 0, c)
                    with dve.Fori(along, TRIPLES) as p:
                        for c in range(RING):
                            add_attention(b, along, p, c)

        @block.tensor
        def _(pe):
            for s in (v_summed, e_summed, c_summed, p_turned, o_summed):
                pe.sem_inc(s, START[s])
            pe.wait_ge(kq_padded, 1)
            pe.wait_ge(w_hi_made, 2)
            pe.wait_ge(w_lo_made, 2)

            def project_v(b, p, c, s):
                j, t = c % 2, TILES * c + s
                pe.wait_ge(v_evicted, past(v_evicted, b * (TILES * CHUNKS) + p * (2 * TILES) + t - 1))
                at = slice(s * P, (s + 1) * P)
                for ct in range(CT):
                    for n, (lo, w) in enumerate(((0, Wv_hi), (0, Wv_lo), (1, Wv_hi))):
                        last = nc.tensor.matmul(v_ps[t % 2][:, :], x_split[:, j, lo, ct, at], w[:, ct, :],
                                                start=(ct == 0 and n == 0), stop=(ct == CT - 1 and n == 2))
                last.then_inc(v_summed, 1)

            def project_kq(b, p, c):
                j = c % 2
                pe.wait_ge(x_hi_made, b * CHUNKS + p * 2 + c + 1)
                pe.wait_ge(x_lo_made, b * CHUNKS + p * 2 + c + 1)
                pe.wait_ge(kq_evicted, past(kq_evicted, b * SUBS + p * 4 + 2 * (c - 1)))
                for ct in range(CT):
                    for n, (w, lo) in enumerate(((Wqk_hi, 0), (Wqk_hi, 1), (Wqk_lo, 0))):
                        last = nc.tensor.matmul(kq_ps[j][:, 0:CP], w[:, ct, :], x_split[:, j, lo, ct, :],
                                                start=(ct == 0 and n == 0), stop=(ct == CT - 1 and n == 2))
                last.then_inc(kq_summed, 1)

            def row_energies(b, p, c):
                pe.wait_ge(kq_evicted, past(kq_evicted, b * SUBS + p * 4 + c + 1))
                pe.wait_ge(e_shifted, past(e_shifted, b * SUBS + p * 4 + c - 1))
                for r in range(SUB):
                    at = slice(r * N, (r + 1) * N)
                    last = nc.tensor.matmul(e_ps[c % 2][0:N, at], kq[:, 1, at], kq[:, 0, at], start=True, stop=True)
                last.then_inc(e_summed, 1)

            def column_energies(b, p, c):
                pe.wait_ge(c_shifted, past(c_shifted, b * GROUPS + p * RING + c - 2))
                for v in range(2):
                    pe.wait_ge(q_gathered, 2 * (b * GROUPS + p * RING + c) + v + 1)
                    for r in range(2):
                        at = (2 * v + r) * N
                        k = KQ[:, :].rearrange("p (h w) -> p h w", w=N)[:, :, (p * RING + c) * GROUP + 2 * v + r]
                        last = nc.tensor.matmul(ce_ps[c][0:N, at:at + N], kq[:, v, r * N:(r + 1) * N], k,
                                                start=True, stop=True)
                    last.then_inc(c_summed, 1)

            def turn(b, along, p, c):
                g = g_no(b, along, p, c)
                pe.wait_ge(p_scaled, g + 1)
                pe.wait_ge(pt_made, past(pt_made, g - 2))
                for r in range(ROWS):
                    last = nc.tensor.transpose(t_ps[c][0:N, r * N:(r + 1) * N], Pe[:, c, r, :], ident[:, :])
                last.then_inc(p_turned, 1)

            def attend(b, along, p, c):
                g = g_no(b, along, p, c)
                pe.wait_ge(pt_made, past(pt_made, g + 1))
                pe.wait_ge(v_in[c], 16 * (b * (2 * TRIPLES) + along * TRIPLES + p + 1))
                for r in range(ROWS):
                    pe.wait_ge(o_added, past(o_added, g * ROWS + r - 3))
                    for ct in range(CT):
                        last = nc.tensor.matmul(o_ps[r][:, ct * WIDE:(ct + 1) * WIDE],
                                                V[:, c, r, ct * P:(ct + 1) * P], Pt[:, c, r * N:r * N + WIDE],
                                                start=True, stop=True)
                    last.then_inc(o_summed, 1)

            with pe.Fori(0, B) as b:
                pe.wait_ge(o_added, past(o_added, b * (2 * CHUNKS * ROWS)))

                def step(p, c):
                    project_kq(b, p, c)
                    project_v(b, p, c, 0)
                    project_v(b, p, c, 1)
                    row_energies(b, p, 2 * c)
                    project_v(b, p, c, 2)
                    row_energies(b, p, 2 * c + 1)

                for c in range(2):
                    step(0, c)
                with pe.Fori(1, PAIRS) as p:
                    for c in range(2):
                        step(p, c)

                pe.wait_ge(e_shifted, past(e_shifted, (b + 1) * SUBS))
                for c in range(RING):
                    column_energies(b, 0, c)
                with pe.Fori(1, TRIPLES) as p:
                    for c in range(RING):
                        column_energies(b, p, c)

                pe.wait_ge(ident_made, (b + 1) * 2)
                pe.wait_ge(z_summed, (b + 1) * (SUBS + GROUPS))
                nc.tensor.transpose(t_ps[0][0:N, 0:N], mx[:, 1, :], ident[:, :])
                nc.tensor.transpose(t_ps[0][0:N, N:2 * N], zs[:, 1, :], ident[:, :]).then_inc(st_turned, 1)
                pe.wait_ge(f_turned, b * 4 + 3)
                nc.tensor.transpose(t_ps[1][0:N, 0:N], st[:, 3, :], ident[:, :]).then_inc(f_turned, 1)

                pe.wait_ge(pads_made, (b + 1) * 5)
                for along in range(2):
                    turn(b, along, 0, 0)
                    with pe.Fori(0, TRIPLES - 1) as p:
                        for c in range(RING):
                            turn(b, along, p + (c + 1) // RING, (c + 1) % RING)
                            attend(b, along, p, c)
                    for c in range(RING):
                        if c < RING - 1:
                            turn(b, along, TRIPLES - 1, c + 1)
                        attend(b, along, TRIPLES - 1, c)


def kernel(**inputs):
    import numpy as np
    import concourse.bacc as bacc
    from concourse.bass_utils import run_bass_kernel_spmd

    w = {k: np.asarray(v) for k, v in inputs.items()}
    arrays = {
        "x": w["x"],
        "wqk_t": np.ascontiguousarray(np.concatenate([w["L0_conv_Wk"], w["L0_conv_Wq"]], 0).T),
        "wv_t": np.ascontiguousarray(w["L0_conv_Wv"].T),
        "bqk": np.concatenate([w["L0_conv_bk"], w["L0_conv_bq"]])[:, None],
        "bv": w["L0_conv_bv"][None, :],
        "gamma": w["L0_conv_gamma"][None, :],
    }
    nc = bacc.Bacc("TRN2", target_bir_lowering=False, num_devices=1)
    args = [nc.dram_tensor(f"in_{k}", a.shape, F32, kind="ExternalInput").ap() for k, a in arrays.items()]
    out = nc.dram_tensor("out", w["x"].shape, F32, kind="ExternalOutput").ap()
    criss_cross_attention(nc, *args, out)
    r = run_bass_kernel_spmd(nc, [{f"in_{k}": a for k, a in arrays.items()}], core_ids=[0])
    return r.results[0]["out"]
```

```python
from contextlib import ExitStack

import concourse.bass as bass
from concourse import mybir

ALU = mybir.AluOpType
ACT = mybir.ActivationFunctionType
AX_X = mybir.AxisListType.X
F32 = mybir.dt.float32
F32R = mybir.dt.float32r

P = 128
N = 96
POS = N * N
ROWS = 4
CP = ROWS * N
CHUNKS = N // ROWS
PAIRS = CHUNKS // 2
TILES = CP // P
SUB = 2
SP_ = SUB * N
SUBS = N // SUB
ERING = 4
GROUP = 4
GROUPS = N // GROUP
RING = 3
TRIPLES = CHUNKS // RING
HALVES = 2
WIDE = 128


def criss_cross_attention(nc, x, wqk_t, wv_t, bqk, bv, gamma, out):
    B, C = x.shape[0], x.shape[1]
    CT = C // P
    CQ = wqk_t.shape[1] // 2
    assert x.shape[2] == N and x.shape[3] == N and C % P == 0 and 2 * CQ == P and CP % P == 0

    v_dram = nc.dram_tensor("v_scratch", (B, POS, C), F32, kind="Internal").ap()
    kq_dram = nc.dram_tensor("kq_scratch", (B, 2, CQ, POS), F32, kind="Internal").ap()
    e_dram = nc.dram_tensor("e_scratch", (2, B, N, N, N), F32, kind="Internal").ap()

    x_v = x.rearrange("b (t p) h w -> b p t (h w)", p=P)
    out_v = out.rearrange("b (t p) h w -> b p t (h w)", p=P)
    v_by_column = v_dram.rearrange("b (g w) c -> b g w c", g=N)
    v_by_row = v_dram.rearrange("b (h u) c -> b u h c", h=N)

    ctx = ExitStack()
    with ctx:
        def sb(name, shape, dt=F32, at=None):
            return (at or ctx).enter_context(nc.sbuf_tensor(name, shape, dt))

        def sem(name):
            return ctx.enter_context(nc.semaphore(name))

        X = sb("X", [P, CT, POS])
        Wv_hi = sb("Wv_hi", [P, CT, C], F32R)
        Wv_lo = sb("Wv_lo", [P, CT, C], F32R)
        Wqk_hi = sb("Wqk_hi", [P, CT, P], F32R)
        Wqk_lo = sb("Wqk_lo", [P, CT, P], F32R)
        bqk_sb = sb("bqk_sb", [P, 1])
        gamma_sb = sb("gamma_sb", [P, 1])
        kq = sb("kq", [P, 2, SP_])
        E = sb("E", [N, RING * GROUP, N])
        E_rows = E[:, 0:ERING * SUB, :].rearrange("p (e r) n -> p e r n", r=SUB)
        E_cols = E[:, :, :].rearrange("p (e r) n -> p e r n", r=GROUP)
        mx = sb("mx", [N, 2, N])
        zs = sb("zs", [N, 2, N])
        with ExitStack() as s1:
            x_split = sb("x_split", [P, 2, 2, CT, CP], F32R, s1)
            ident_ = sb("ident_", [N, N], F32, s1)
            gap = sb("gap", [P, POS - 4 * CT * CP - N - (TILES + 1) * C], F32, s1)
            v_out = sb("v_out", [P, TILES, C], F32, s1)
            bv_row = sb("bv_row", [P, C], F32, s1)
        with ExitStack() as s2:
            KQ = sb("KQ", [P, POS], F32, s2)
        with ExitStack() as s3:
            V = sb("V", [P, RING, ROWS, C], F32, s3)
            ident = sb("ident", [N, N], F32, s3)
            Pe = sb("Pe", [N, RING, ROWS, N], F32, s3)
            Pt = sb("Pt", [P, RING, CP + WIDE - N], F32, s3)
            st = sb("st", [N, 4, N], F32, s3)
        slot_rows = 2 * CT * CP // N
        ident_row = 2 * slot_rows
        gap_rows = (gap.shape[1]) // N

        bank = [ctx.enter_context(nc.psum_tensor(f"bank{i}", [P, 512], F32)) for i in range(8)]
        v_ps, kq_ps, e_ps = bank[0:2], bank[2:4], bank[4:6]
        ce_ps = bank[5:8]
        t_ps, f_ps, o_ps = bank[2:5], bank[5], bank[6:8] + bank[0:2]

        halves = [slice(h * CT // HALVES, (h + 1) * CT // HALVES) for h in range(HALVES)]
        RAW_V, RAW_QK = slice(POS - CT * C, POS), slice(POS - CT * P, POS)

        wqk_in = sem("wqk_in")
        wv_in = sem("wv_in")
        small_in = sem("small_in")
        kq_padded = sem("kq_padded")
        w_hi_made = sem("w_hi_made")
        w_lo_made = sem("w_lo_made")
        x_in = [sem(f"x_in{j}") for j in range(2)]
        bv_in = sem("bv_in")
        x_hi_made = sem("x_hi_made")
        x_lo_made = sem("x_lo_made")
        v_summed = sem("v_summed")
        v_evicted = sem("v_evicted")
        v_stored = [sem(f"v_stored{j}") for j in range(TILES)]
        kq_summed = sem("kq_summed")
        kq_evicted = sem("kq_evicted")
        kq_stored = sem("kq_stored")
        sync_stages = sem("sync_stages")
        kq_in = sem("kq_in")
        e_summed = sem("e_summed")
        e_maxed = sem("e_maxed")
        e_shifted = sem("e_shifted")
        e_exped = sem("e_exped")
        e_stored = [sem(f"e_stored{j}") for j in range(ERING)]
        q_gathered = sem("q_gathered")
        c_summed = sem("c_summed")
        c_maxed = sem("c_maxed")
        c_shifted = sem("c_shifted")
        c_exped = sem("c_exped")
        pool_passed = sem("pool_passed")
        c_masked = sem("c_masked")
        c_stored = [sem(f"c_stored{j}") for j in range(RING)]
        z_summed = sem("z_summed")
        ident_made = sem("ident_made")
        st_turned = sem("st_turned")
        st_step = sem("st_step")
        st_exped = sem("st_exped")
        f_turned = sem("f_turned")
        f_made = sem("f_made")
        v_in = [sem(f"v_in{j}") for j in range(RING)]
        p_in = [sem(f"p_in{j}") for j in range(RING)]
        pt_padded = sem("pt_padded")
        v_padded = [sem(f"v_padded{j}") for j in range(RING)]
        p_scaled = sem("p_scaled")
        p_turned = sem("p_turned")
        pt_made = sem("pt_made")
        o_summed = sem("o_summed")
        o_added = sem("o_added")
        out_stored = [sem(f"out_stored{j}") for j in range(2)]

        def g_no(b, along, p, c):
            return b * (2 * CHUNKS) + CHUNKS * along + p * RING + c

        ST_STEPS = 8

        START = {x_in[0]: 16, x_in[1]: 16, kq_stored: 16, **{s: 16 for s in v_stored + e_stored + c_stored},
                 out_stored[0]: 16 * PAIRS, out_stored[1]: 16 * PAIRS,
                 kq_evicted: 3, v_evicted: 2, v_summed: TILES + 1, e_shifted: 2, c_shifted: 3, e_summed: 1,
                 c_summed: 2, pt_made: 3, p_turned: 3, o_summed: 2 * ROWS + 1, o_added: 4}

        def past(s, n):
            return n + START[s]

        block = ctx.enter_context(nc.Block())

        @block.sync
        def _(sp):
            for s in (*x_in, *v_stored, kq_stored, *e_stored, *c_stored, *out_stored):
                sp.sem_inc(s, START[s])
            def load_x(b, p, c):
                j, n = c % 2, p + c // 2
                sp.wait_ge(x_in[j], past(x_in[j], 16 * (b * PAIRS + n)))
                sp.wait_ge(out_stored[j], past(out_stored[j], 16 * ((b - 1) * PAIRS + n + 1)))
                at = bass.ds((p * 2 + c) * CP, CP)
                sp.dma_start(X[:, :, at], x_v[b, :, :, at]).then_inc(x_in[j], 16)

            def store_v(b, p, c, s):
                sp.wait_ge(v_evicted, past(v_evicted, b * (TILES * CHUNKS) + p * (2 * TILES) + TILES * c + s + 1))
                sp.dma_start(v_dram[b, bass.ds(p * (2 * CP) + (TILES * c + s) * P, P), :], v_out[:, s, :])\
                    .then_inc(v_stored[s], 16)

            def store_kq(b, p, c, v):
                u = 2 * c + v
                sp.wait_ge(kq_evicted, past(kq_evicted, b * SUBS + p * 4 + u + 1))
                sp.dma_start(kq_dram[b, :, :, bass.ds((p * 4 + u) * SP_, SP_)].rearrange("t c n -> c t n"),
                             kq[0:CQ, :, :]).then_inc(kq_stored, 16)

            def store_e(b, p, c, v):
                u = 2 * c + v
                sp.wait_ge(e_exped, b * SUBS + p * 4 + u + 1)
                sp.dma_start(e_dram[1, b, :, bass.ds((p * 4 + u) * SUB, SUB), :], E_rows[:, u % ERING, :, :])\
                    .then_inc(e_stored[u % ERING], 16)

            def load_kq(b, first_row, rows):
                at = slice(first_row * N, (first_row + rows) * N)
                sp.dma_start(KQ[:, at], kq_dram[b, :, :, at].rearrange("t c n -> (t c) n")).then_inc(kq_in, 16)

            def store_c(b, p, c):
                sp.wait_ge(c_masked, b * GROUPS + p * RING + c + 1)
                sp.dma_start(e_dram[0, b, :, bass.ds((p * RING + c) * GROUP, GROUP), :], E_cols[:, c, :, :])\
                    .then_inc(c_stored[c], 16)

            def load_attention(b, along, p, c, free=False):
                g = g_no(b, along, p, c)
                at = bass.ds((p * RING + c) * ROWS, ROWS)
                if not free:
                    sp.wait_ge(p_turned, past(p_turned, g - 2))
                sp.dma_start(Pe[:, c, :, :], e_dram[along, b, :, at, :]).then_inc(p_in[c], 16)
                if not free:
                    sp.wait_ge(o_summed, past(o_summed, (g - 2) * ROWS))
                sp.dma_start(V[0:N, c, :, :], (v_by_row if along else v_by_column)[b, :, at, :])\
                    .then_inc(v_in[c], 16)

            def store_out(b, p, c):
                sp.wait_ge(o_added, past(o_added, (b * (2 * CHUNKS) + CHUNKS + p * 2 + c + 1) * ROWS))
                at = bass.ds((p * 2 + c) * CP, CP)
                sp.dma_start(out_v[b, :, :, at], X[:, :, at]).then_inc(out_stored[c % 2], 16)

            def next_x(b, p, c, drains):
                load_x(b, p, c)
                if drains:
                    store_out(b - 1, p, c + 2)

            def first_stage(b, drains):
                next_x(b, 0, 2, drains)
                sp.wait_ge(o_summed, past(o_summed, b * (2 * CHUNKS * ROWS)))
                sp.dma_start(bv_row[:, :], bv.to_broadcast((P, C))).then_inc(bv_in, 16)

                def stores(p, c, drains=False, x_too=True):
                    store_kq(b, p, c, 0)
                    if x_too:
                        next_x(b, p, c + 3, drains)
                    store_v(b, p, c, 0)
                    store_v(b, p, c, 1)
                    store_kq(b, p, c, 1)
                    store_e(b, p, c, 0)
                    store_v(b, p, c, 2)
                    store_e(b, p, c, 1)

                with sp.Fori(0, PAIRS - 3) as p:
                    for c in range(2):
                        stores(p, c, drains)
                for c in range(3):
                    stores(PAIRS - 3, c, drains and c == 0)
                for c in range(3, 5):
                    stores(PAIRS - 3, c, x_too=False)
                sp.wait_ge(v_summed, past(v_summed, (b + 1) * (TILES * CHUNKS) - TILES))
                sp.sem_inc(sync_stages, 1)
                load_kq(b, 0, slot_rows)
                store_kq(b, PAIRS - 1, 1, 0)
                store_v(b, PAIRS - 1, 1, 0)
                load_kq(b, ident_row + 1, gap_rows)
                store_v(b, PAIRS - 1, 1, 1)
                store_kq(b, PAIRS - 1, 1, 1)
                store_e(b, PAIRS - 1, 1, 0)
                store_v(b, PAIRS - 1, 1, 2)
                sp.wait_ge(v_summed, past(v_summed, (b + 1) * (TILES * CHUNKS)))
                sp.sem_inc(sync_stages, 1)
                load_kq(b, slot_rows, slot_rows)
                store_e(b, PAIRS - 1, 1, 1)

            def other_stages(b, last):
                for s in range(TILES):
                    sp.wait_ge(v_stored[s], past(v_stored[s], (b + 1) * (16 * CHUNKS)))
                sp.sem_inc(sync_stages, 1)
                sp.wait_ge(kq_stored, past(kq_stored, (b + 1) * (16 * SUBS)))
                load_kq(b, ident_row + 1 + gap_rows, N - ident_row - 1 - gap_rows)
                sp.wait_ge(st_turned, b + 1)
                load_kq(b, ident_row, 1)
                with sp.Fori(0, TRIPLES - 1) as p:
                    for c in range(RING):
                        store_c(b, p, c)
                store_c(b, TRIPLES - 1, 0)
                sp.wait_ge(c_summed, past(c_summed, (b + 1) * (2 * GROUPS)))
                sp.sem_inc(sync_stages, 1)
                load_attention(b, 0, 0, 0, free=True)
                store_c(b, TRIPLES - 1, 1)
                load_attention(b, 0, 0, 1, free=True)
                store_c(b, TRIPLES - 1, 2)
                load_attention(b, 0, 0, 2, free=True)
                for j in range(ERING):
                    sp.wait_ge(e_stored[j], past(e_stored[j], (b + 1) * (16 * SUBS // ERING)))
                sp.sem_inc(sync_stages, 1)
                for j in range(RING):
                    sp.wait_ge(c_stored[j], past(c_stored[j], (b + 1) * (16 * TRIPLES)))
                sp.sem_inc(sync_stages, 1)
                with sp.Fori(1, TRIPLES) as p:
                    for c in range(RING):
                        load_attention(b, 0, p, c)
                if last:
                    for c in range(RING):
                        load_attention(b, 1, 0, c)
                    with sp.Fori(0, CHUNKS // (2 * RING) - 1) as p:
                        for c in range(2 * RING):
                            load_attention(b, 1, p * 2 + 1 + c // RING, c % RING)
                            store_out(b, p * RING, c)
                    for c in range(RING):
                        load_attention(b, 1, TRIPLES - 1, c)
                        store_out(b, PAIRS - RING, c)
                    for c in range(RING):
                        store_out(b, PAIRS - RING, RING + c)
                else:
                    with sp.Fori(0, TRIPLES - 3) as p:
                        for c in range(RING):
                            load_attention(b, 1, p, c)
                    leaves, comes = (0, 2, 5, 8), (4, 7)
                    for n in range(3 * RING):
                        load_attention(b, 1, TRIPLES - 3 + n // RING, n % RING)
                        if n in leaves:
                            store_out(b, 0, leaves.index(n))
                        if n in comes:
                            load_x(b + 1, 0, comes.index(n))

            load_x(0, 0, 0)
            sp.dma_start(X[:, 1, RAW_QK].rearrange("p (t n) -> p t n", t=CT),
                         wqk_t.rearrange("(t p) n -> p t n", p=P)).then_inc(wqk_in, 16)
            sp.dma_start(bqk_sb[:, :], bqk).then_inc(small_in, 16)
            sp.dma_start(gamma_sb[:, :], gamma.to_broadcast((P, 1))).then_inc(small_in, 16)
            sp.dma_start(X[:, 0, RAW_V].rearrange("p (t n) -> p t n", t=CT),
                         wv_t.rearrange("(t p) n -> p t n", p=P)).then_inc(wv_in, 16)
            load_x(0, 0, 1)
            sp.wait_ge(w_hi_made, 2)
            sp.wait_ge(w_lo_made, 2)
            first_stage(0, False)
            with sp.Fori(0, B - 1) as b:
                other_stages(b, False)
                first_stage(b + 1, True)
            other_stages(B - 1, True)
            for j in range(2):
                sp.wait_ge(out_stored[j], past(out_stored[j], 16 * PAIRS * B))

        @block.gpsimd
        def _(pool):
            def split_x(b, p, c):
                for h, cts in enumerate(halves):
                    pool.wait_ge(x_hi_made, (b * CHUNKS + p * 2 + c) * HALVES + h + 1)
                    nc.gpsimd.tensor_tensor(x_split[:, c % 2, 1, cts, :], X[:, cts, bass.ds((p * 2 + c) * CP, CP)],
                                            x_split[:, c % 2, 0, cts, :].bitcast(F32), ALU.subtract)\
                        .then_inc(x_lo_made, 1)

            def mask(b, p, c):
                pool.wait_ge(c_exped, b * GROUPS + p * RING + c + 1)
                pool.sem_inc(pool_passed, 1)
                nc.gpsimd.affine_select(out=E_cols[:, c, :, :], in_=E_cols[:, c, :, :], compare_op=ALU.not_equal,
                                        fill=0.0, base=0, pattern=[[0, GROUP], [-1, N]], channel_multiplier=1)\
                    .then_inc(c_masked, 1)

            def scale(b, along, p, c):
                pool.wait_ge(p_in[c], 16 * (b * (2 * TRIPLES) + along * TRIPLES + p + 1))
                f = mx[:, along, bass.ds((p * RING + c) * ROWS, ROWS)].unsqueeze(2).to_broadcast((N, ROWS, N))
                nc.gpsimd.tensor_tensor(Pe[:, c, :, :], Pe[:, c, :, :], f, ALU.mult)\
                    .then_inc(p_scaled, 1)

            def make_ident(times_before):
                nc.gpsimd.memset(ident[:, :], 0.0).then_inc(ident_made, 1)
                pool.wait_ge(ident_made, times_before * 2 + 1)
                pool.sem_inc(pool_passed, 1)
                nc.gpsimd.affine_select(out=ident[:, :], in_=ident[:, :], compare_op=ALU.not_equal, fill=1.0,
                                        base=0, pattern=[[-1, N]], channel_multiplier=1).then_inc(ident_made, 1)

            make_ident(0)
            with pool.Fori(0, B) as b:
                with pool.Fori(0, PAIRS) as p:
                    for c in range(2):
                        split_x(b, p, c)
                with pool.Fori(0, TRIPLES - 1) as p:
                    for c in range(RING):
                        mask(b, p, c)
                mask(b, TRIPLES - 1, 0)
                pool.wait_ge(c_summed, past(c_summed, (b + 1) * (2 * GROUPS)))
                pool.sem_inc(pool_passed, 1)
                make_ident(b + 1)
                mask(b, TRIPLES - 1, 1)
                mask(b, TRIPLES - 1, 2)
                nc.gpsimd.memset(Pt[0:N, :, CP:], 0.0).then_inc(pt_padded, 1)
                nc.gpsimd.memset(Pt[N:P, :, :], 0.0).then_inc(pt_padded, 1)
                nc.gpsimd.memset(V[N:P, 0, :, :], 0.0).then_inc(v_padded[0], 1)
                for along in range(2):
                    pool.wait_ge(f_made, b * 2 + along + 1)
                    pool.sem_inc(pool_passed, 1)
                    with pool.Fori(0, TRIPLES) as p:
                        for c in range(RING):
                            scale(b, along, p, c)

        @block.scalar
        def _(act):
            act.sem_inc(kq_evicted, START[kq_evicted])
            act.sem_inc(pt_made, START[pt_made])
            def round_x(b, p, c):
                j, n = c % 2, p + c // 2
                act.wait_ge(x_in[j], past(x_in[j], 16 * (b * PAIRS + n + 1)))
                act.wait_ge(v_summed, past(v_summed, (b * CHUNKS + p * 2 + c - 1) * TILES))
                for cts in halves:
                    nc.scalar.activation(x_split[:, j, 0, cts, :], X[:, cts, bass.ds((p * 2 + c) * CP, CP)],
                                         ACT.Copy).then_inc(x_hi_made, 1)

            def evict_kq(b, p, c, v):
                u = 2 * c + v
                act.wait_ge(kq_summed, b * CHUNKS + p * 2 + c + 1)
                act.wait_ge(e_summed, past(e_summed, b * SUBS + p * 4 + u))
                act.wait_ge(kq_stored, past(kq_stored, 16 * (b * SUBS + p * 4 + u)))
                for i in range(2):
                    rows = slice(i * CQ, (i + 1) * CQ)
                    last = nc.scalar.activation(kq[0:CQ, i, :], kq_ps[c % 2][rows, v * SP_:(v + 1) * SP_],
                                                ACT.Identity, bias=bqk_sb[rows, :])
                last.then_inc(kq_evicted, 1)

            def exponentials(b, p, c):
                act.wait_ge(e_shifted, past(e_shifted, b * SUBS + p * 4 + c + 1))
                nc.scalar.activation(E_rows[:, c % ERING, :, :], E_rows[:, c % ERING, :, :], ACT.Exp)\
                    .then_inc(e_exped, 1)

            def gather_q(b, p, c, v):
                u = (p * RING + c) * 2 + v
                act.wait_ge(c_summed, past(c_summed, b * (2 * GROUPS) + u - 1))
                src = KQ[CQ:2 * CQ, :].rearrange("p (h w) -> p w h", w=N)[:, bass.ds(u * 2, 2), :]
                nc.scalar.activation(kq[0:CQ, v, :].rearrange("p (w h) -> p w h", w=2), src, ACT.Copy)\
                    .then_inc(q_gathered, 1)

            def exponentials_c(b, p, c):
                act.wait_ge(c_shifted, past(c_shifted, b * GROUPS + p * RING + c + 1))
                nc.scalar.activation(E_cols[:, c % RING, :, :], E_cols[:, c % RING, :, :], ACT.Exp)\
                    .then_inc(c_exped, 1)

            def copy_turned(b, along, p, c):
                g = g_no(b, along, p, c)
                act.wait_ge(p_turned, past(p_turned, g + 1))
                act.wait_ge(o_summed, past(o_summed, (g - 2) * ROWS))
                nc.scalar.activation(Pt[0:N, c, 0:CP], t_ps[c][0:N, 0:CP], ACT.Copy)\
                    .then_inc(pt_made, 1)

            act.wait_ge(wqk_in, 16)
            nc.scalar.activation(Wqk_hi[:, :, :], X[:, 1, RAW_QK].rearrange("p (t n) -> p t n", t=CT),
                                 ACT.Copy).then_inc(w_hi_made, 1)
            act.wait_ge(small_in, 32)
            with act.Fori(0, B) as b:
                act.wait_ge(o_summed, past(o_summed, b * (2 * CHUNKS * ROWS) - ROWS))
                round_x(b, 0, 0)
                act.wait_ge(o_summed, past(o_summed, b * (2 * CHUNKS * ROWS)))
                round_x(b, 0, 1)

                def step(p, c, more):
                    evict_kq(b, p, c, 0)
                    if more:
                        round_x(b, p, c + 1)
                    evict_kq(b, p, c, 1)
                    exponentials(b, p, 2 * c)
                    exponentials(b, p, 2 * c + 1)

                step(0, 0, False)
                step(0, 1, True)
                with act.Fori(1, PAIRS - 1) as p:
                    for c in range(2):
                        step(p, c, True)
                for c in range(2):
                    step(PAIRS - 1, c, c == 0)

                act.wait_ge(kq_in, 16 * 5 * (b + 1))
                for c in range(RING):
                    for v in range(2):
                        gather_q(b, 0, c, v)
                with act.Fori(0, TRIPLES - 1) as p:
                    for c in range(RING, 2 * RING):
                        gather_q(b, p, c, 0)
                        exponentials_c(b, p, c - RING)
                        gather_q(b, p, c, 1)
                for c in range(RING):
                    exponentials_c(b, TRIPLES - 1, c)

                act.wait_ge(st_step, b * ST_STEPS + 3)
                nc.scalar.activation(st[:, 1:3, :], st[:, 1:3, :], ACT.Exp).then_inc(st_exped, 1)
                for j in (1, 2):
                    nc.scalar.activation(V[N:P, j, :, :].rearrange("p r c -> p (r c)"),
                                         kq[N:P, 0, 0:1].to_broadcast((P - N, ROWS * C)), ACT.Copy)\
                        .then_inc(v_padded[j], 1)

                for along in range(2):
                    with act.Fori(0, TRIPLES) as p:
                        for c in range(RING):
                            copy_turned(b, along, p, c)

        @block.vector
        def _(dve):
            dve.sem_inc(v_evicted, START[v_evicted])
            dve.sem_inc(e_shifted, START[e_shifted])
            dve.sem_inc(c_shifted, START[c_shifted])
            dve.sem_inc(o_added, START[o_added])
            nc.vector.memset(kq[CQ:P, :, :], 0.0).then_inc(kq_padded, 1)
            dve.wait_ge(w_hi_made, 1)
            nc.vector.tensor_tensor(Wqk_lo[:, :, :], X[:, 1, RAW_QK].rearrange("p (t n) -> p t n", t=CT),
                                    Wqk_hi[:, :, :].bitcast(F32), ALU.subtract).then_inc(w_lo_made, 1)
            dve.wait_ge(wv_in, 16)
            nc.vector.tensor_copy(Wv_hi[:, :, :], X[:, 0, RAW_V].rearrange("p (t n) -> p t n", t=CT))\
                .then_inc(w_hi_made, 1)
            dve.wait_ge(w_hi_made, 2)
            nc.vector.tensor_tensor(Wv_lo[:, :, :], X[:, 0, RAW_V].rearrange("p (t n) -> p t n", t=CT),
                                    Wv_hi[:, :, :].bitcast(F32), ALU.subtract).then_inc(w_lo_made, 1)

            def evict_v(b, p, c, s):
                t = TILES * c + s
                dve.wait_ge(v_summed, past(v_summed, b * (TILES * CHUNKS) + p * (2 * TILES) + t + 1))
                dve.wait_ge(v_stored[s], past(v_stored[s], 16 * (b * CHUNKS + p * 2 + c)))
                nc.vector.tensor_tensor(v_out[:, s, :], v_ps[t % 2][:, :], bv_row[:, :], ALU.add)\
                    .then_inc(v_evicted, 1)

            def shift(b, p, c):
                e = b * SUBS + p * 4 + c
                ps = e_ps[c % 2][0:N, 0:SP_].rearrange("p (r n) -> p r n", r=SUB)
                m = mx[:, 1, bass.ds((p * 4 + c) * SUB, SUB)]
                dve.wait_ge(e_summed, past(e_summed, e + 1))
                nc.vector.tensor_reduce(m, ps, AX_X, ALU.max).then_inc(e_maxed, 1)
                dve.wait_ge(e_stored[c % ERING], past(e_stored[c % ERING], 16 * (b * (SUBS // ERING) + p + c // ERING)))
                dve.wait_ge(e_maxed, e + 1)
                nc.vector.tensor_tensor(E_rows[:, c % ERING, :, :], ps, m.unsqueeze(2).to_broadcast((N, SUB, N)),
                                        ALU.subtract).then_inc(e_shifted, 1)

            def sum_z(b, p, c):
                dve.wait_ge(e_exped, b * SUBS + p * 4 + c + 1)
                nc.vector.tensor_reduce(zs[:, 1, bass.ds((p * 4 + c) * SUB, SUB)], E_rows[:, c % ERING, :, :],
                                        AX_X, ALU.add).then_inc(z_summed, 1)

            def group_of(p, c):
                ps = ce_ps[c % RING][0:N, 0:GROUP * N].rearrange("p (r n) -> p r n", r=GROUP)
                return ps, mx[:, 0, bass.ds((p * RING + c) * GROUP, GROUP)]

            def max_c(b, p, c):
                ps, m = group_of(p, c)
                dve.wait_ge(c_summed, past(c_summed, 2 * (b * GROUPS + p * RING + c + 1)))
                nc.vector.tensor_reduce(m, ps, AX_X, ALU.max).then_inc(c_maxed, 1)

            def shift_c(b, p, c):
                ps, m = group_of(p, c)
                dve.wait_ge(c_stored[c % RING], past(c_stored[c % RING], 16 * (b * TRIPLES + p + c // RING)))
                dve.wait_ge(c_maxed, b * GROUPS + p * RING + c + 1)
                nc.vector.tensor_tensor(E_cols[:, c % RING, :, :], ps, m.unsqueeze(2).to_broadcast((N, GROUP, N)),
                                        ALU.subtract).then_inc(c_shifted, 1)

            def sum_c(b, p, c):
                dve.wait_ge(c_masked, b * GROUPS + p * RING + c + 1)
                nc.vector.tensor_reduce(zs[:, 0, bass.ds((p * RING + c) * GROUP, GROUP)], E_cols[:, c % RING, :, :],
                                        AX_X, ALU.add).then_inc(z_summed, 1)

            def add_attention(b, along, p, c):
                for r in range(ROWS):
                    n = g_no(b, along, p, c) * ROWS + r
                    dve.wait_ge(o_summed, past(o_summed, n + 1))
                    at = (p * RING + c) * ROWS + r
                    if along:
                        xs = X[:, :, bass.ds(at * N, N)]
                    else:
                        xs = X[:, :, :].rearrange("p t (h w) -> p t h w", w=N)[:, :, :, at]
                    nc.vector.tensor_tensor(xs, o_ps[r][:, :].rearrange("p (t n) -> p t n", t=CT)[:, :, 0:N], xs,
                                            ALU.add).then_inc(o_added, 1)

            with dve.Fori(0, B) as b:
                dve.wait_ge(bv_in, 16 * (b + 1))

                def step(p, c):
                    evict_v(b, p, c, 0)
                    evict_v(b, p, c, 1)
                    shift(b, p, 2 * c)
                    evict_v(b, p, c, 2)
                    sum_z(b, p, 2 * c)
                    shift(b, p, 2 * c + 1)
                    sum_z(b, p, 2 * c + 1)

                for c in range(2):
                    step(0, c)
                with dve.Fori(1, PAIRS) as p:
                    for c in range(2):
                        step(p, c)

                max_c(b, 0, 0)
                for j in range(ERING):
                    dve.wait_ge(e_stored[j], past(e_stored[j], 16 * (b + 1) * (SUBS // ERING)))
                for c in range(1, 4):
                    if c == 3:
                        sum_c(b, 0, 0)
                    max_c(b, 0, c)
                    shift_c(b, 0, c - 1)
                with dve.Fori(0, TRIPLES - 2) as p:
                    for c in range(4, 4 + RING):
                        sum_c(b, p, c - 3)
                        max_c(b, p, c)
                        shift_c(b, p, c - 1)
                for c in (4, 5):
                    sum_c(b, TRIPLES - 2, c - 3)
                    max_c(b, TRIPLES - 2, c)
                    shift_c(b, TRIPLES - 2, c - 1)
                sum_c(b, TRIPLES - 1, 0)
                shift_c(b, TRIPLES - 1, 2)

                turned = t_ps[0][0:N, 0:2 * N].rearrange("p (k n) -> p k n", k=2)
                steps = b * ST_STEPS
                dve.wait_ge(st_turned, b + 1)
                dve.wait_ge(c_maxed, (b + 1) * GROUPS)
                nc.vector.tensor_tensor(st[:, 0, :], turned[:, 0, :], mx[:, 0, :], ALU.max).then_inc(st_step, 1)
                dve.wait_ge(st_step, steps + 1)
                nc.vector.tensor_tensor(st[:, 1, :], mx[:, 0, :], st[:, 0, :], ALU.subtract).then_inc(st_step, 1)
                nc.vector.tensor_tensor(st[:, 2, :], turned[:, 0, :], st[:, 0, :], ALU.subtract).then_inc(st_step, 1)
                sum_c(b, TRIPLES - 1, 1)
                dve.wait_ge(st_exped, b + 1)
                nc.vector.tensor_tensor(st[:, 3, :], turned[:, 1, :], st[:, 2, :], ALU.mult).then_inc(st_step, 1)
                sum_c(b, TRIPLES - 1, 2)
                dve.wait_ge(z_summed, (b + 1) * (SUBS + GROUPS))
                nc.vector.tensor_tensor(st[:, 0, :], st[:, 1, :], zs[:, 0, :], ALU.mult).then_inc(st_step, 1)
                dve.wait_ge(st_step, steps + 5)
                nc.vector.tensor_tensor(st[:, 0, :], st[:, 0, :], st[:, 3, :], ALU.add).then_inc(st_step, 1)
                nc.vector.tensor_scalar(st[:, 1:3, :], st[:, 1:3, :], gamma_sb[0:N, 0:1], None, ALU.mult)\
                    .then_inc(st_step, 1)
                dve.wait_ge(st_step, steps + 7)
                nc.vector.reciprocal(st[:, 3, :], st[:, 0, :]).then_inc(st_step, 1)
                dve.wait_ge(st_step, steps + 8)
                nc.vector.tensor_tensor(mx[:, 0, :], st[:, 1, :], st[:, 3, :], ALU.mult).then_inc(f_made, 1)
                nc.vector.tensor_tensor(st[:, 0, :], st[:, 2, :], st[:, 3, :], ALU.mult).then_inc(f_turned, 1)
                dve.wait_ge(f_turned, b * 2 + 2)
                nc.vector.tensor_copy(mx[:, 1, :], f_ps[0:N, 0:N]).then_inc(f_made, 1)

                for along in range(2):
                    if along:
                        dve.wait_ge(o_added, past(o_added, (b * (2 * CHUNKS) + CHUNKS) * ROWS))
                        for c in range(RING):
                            add_attention(b, 1, 0, c)
                    with dve.Fori(along, TRIPLES) as p:
                        for c in range(RING):
                            add_attention(b, along, p, c)

        @block.tensor
        def _(pe):
            for s in (v_summed, e_summed, c_summed, p_turned, o_summed):
                pe.sem_inc(s, START[s])
            pe.wait_ge(kq_padded, 1)
            pe.wait_ge(w_lo_made, 1)

            def project_v(b, p, c, s):
                j, t = c % 2, TILES * c + s
                pe.wait_ge(v_evicted, past(v_evicted, b * (TILES * CHUNKS) + p * (2 * TILES) + t - 1))
                at = slice(s * P, (s + 1) * P)
                for ct in range(CT):
                    for n, (lo, w) in enumerate(((0, Wv_hi), (0, Wv_lo), (1, Wv_hi))):
                        last = nc.tensor.matmul(v_ps[t % 2][:, :], x_split[:, j, lo, ct, at], w[:, ct, :],
                                                start=(ct == 0 and n == 0), stop=(ct == CT - 1 and n == 2))
                last.then_inc(v_summed, 1)

            def project_kq(b, p, c):
                j = c % 2
                pe.wait_ge(kq_evicted, past(kq_evicted, b * SUBS + p * 4 + 2 * (c - 1)))
                for ct in range(CT):
                    if ct % (CT // HALVES) == 0:
                        n = (b * CHUNKS + p * 2 + c) * HALVES + ct // (CT // HALVES) + 1
                        pe.wait_ge(x_hi_made, n)
                        pe.wait_ge(x_lo_made, n)
                    for n, (w, lo) in enumerate(((Wqk_hi, 0), (Wqk_hi, 1), (Wqk_lo, 0))):
                        last = nc.tensor.matmul(kq_ps[j][:, 0:CP], w[:, ct, :], x_split[:, j, lo, ct, :],
                                                start=(ct == 0 and n == 0), stop=(ct == CT - 1 and n == 2))
                last.then_inc(kq_summed, 1)

            def row_energies(b, p, c):
                pe.wait_ge(kq_evicted, past(kq_evicted, b * SUBS + p * 4 + c + 1))
                pe.wait_ge(e_shifted, past(e_shifted, b * SUBS + p * 4 + c - 1))
                for r in range(SUB):
                    at = slice(r * N, (r + 1) * N)
                    last = nc.tensor.matmul(e_ps[c % 2][0:N, at], kq[:, 1, at], kq[:, 0, at], start=True, stop=True)
                last.then_inc(e_summed, 1)

            def column_energies(b, p, c):
                pe.wait_ge(c_shifted, past(c_shifted, b * GROUPS + p * RING + c - 2))
                for v in range(2):
                    pe.wait_ge(q_gathered, 2 * (b * GROUPS + p * RING + c) + v + 1)
                    for r in range(2):
                        at = (2 * v + r) * N
                        k = KQ[:, :].rearrange("p (h w) -> p h w", w=N)[:, :, (p * RING + c) * GROUP + 2 * v + r]
                        last = nc.tensor.matmul(ce_ps[c][0:N, at:at + N], kq[:, v, r * N:(r + 1) * N], k,
                                                start=True, stop=True)
                    last.then_inc(c_summed, 1)

            def turn(b, along, p, c):
                g = g_no(b, along, p, c)
                pe.wait_ge(p_scaled, g + 1)
                pe.wait_ge(pt_made, past(pt_made, g - 2))
                for r in range(ROWS):
                    last = nc.tensor.transpose(t_ps[c][0:N, r * N:(r + 1) * N], Pe[:, c, r, :], ident[:, :])
                last.then_inc(p_turned, 1)

            def attend(b, along, p, c):
                g = g_no(b, along, p, c)
                pe.wait_ge(pt_made, past(pt_made, g + 1))
                pe.wait_ge(v_in[c], 16 * (b * (2 * TRIPLES) + along * TRIPLES + p + 1))
                for r in range(ROWS):
                    pe.wait_ge(o_added, past(o_added, g * ROWS + r - 3))
                    for ct in range(CT):
                        last = nc.tensor.matmul(o_ps[r][:, ct * WIDE:(ct + 1) * WIDE],
                                                V[:, c, r, ct * P:(ct + 1) * P], Pt[:, c, r * N:r * N + WIDE],
                                                start=True, stop=True)
                    last.then_inc(o_summed, 1)

            with pe.Fori(0, B) as b:
                def step(p, c, first=False):
                    project_kq(b, p, c)
                    if first:
                        pe.wait_ge(w_lo_made, 2)
                        pe.wait_ge(o_added, past(o_added, b * (2 * CHUNKS * ROWS)))
                    project_v(b, p, c, 0)
                    project_v(b, p, c, 1)
                    row_energies(b, p, 2 * c)
                    project_v(b, p, c, 2)
                    row_energies(b, p, 2 * c + 1)

                for c in range(2):
                    step(0, c, first=(c == 0))
                with pe.Fori(1, PAIRS) as p:
                    for c in range(2):
                        step(p, c)

                pe.wait_ge(ident_made, (b + 1) * 2)
                pe.wait_ge(z_summed, b * (SUBS + GROUPS) + SUBS)
                nc.tensor.transpose(t_ps[0][0:N, 0:N], mx[:, 1, :], ident[:, :])
                nc.tensor.transpose(t_ps[0][0:N, N:2 * N], zs[:, 1, :], ident[:, :]).then_inc(st_turned, 1)
                pe.wait_ge(e_shifted, past(e_shifted, (b + 1) * SUBS))
                for c in range(RING):
                    column_energies(b, 0, c)
                with pe.Fori(1, TRIPLES) as p:
                    for c in range(RING):
                        column_energies(b, p, c)

                pe.wait_ge(ident_made, (b + 2) * 2)
                pe.wait_ge(f_turned, b * 2 + 1)
                nc.tensor.transpose(f_ps[0:N, 0:N], st[:, 0, :], ident[:, :]).then_inc(f_turned, 1)

                pe.wait_ge(pt_padded, (b + 1) * 2)
                for j in range(RING):
                    pe.wait_ge(v_padded[j], b + 1)
                turn(b, 0, 0, 0)
                for along in range(2):
                    with pe.Fori(0, TRIPLES - 1) as p:
                        for c in range(RING):
                            turn(b, along, p + (c + 1) // RING, (c + 1) % RING)
                            attend(b, along, p, c)
                    for c in range(RING):
                        if c < RING - 1:
                            turn(b, along, TRIPLES - 1, c + 1)
                        elif along == 0:
                            turn(b, 1, 0, 0)
                        attend(b, along, TRIPLES - 1, c)


def kernel(**inputs):
    import numpy as np
    import concourse.bacc as bacc
    from concourse.bass_utils import run_bass_kernel_spmd

    w = {k: np.asarray(v) for k, v in inputs.items()}
    arrays = {
        "x": w["x"],
        "wqk_t": np.ascontiguousarray(np.concatenate([w["L0_conv_Wk"], w["L0_conv_Wq"]], 0).T),
        "wv_t": np.ascontiguousarray(w["L0_conv_Wv"].T),
        "bqk": np.concatenate([w["L0_conv_bk"], w["L0_conv_bq"]])[:, None],
        "bv": w["L0_conv_bv"][None, :],
        "gamma": w["L0_conv_gamma"][None, :],
    }
    nc = bacc.Bacc("TRN2", target_bir_lowering=False, num_devices=1)
    args = [nc.dram_tensor(f"in_{k}", a.shape, F32, kind="ExternalInput").ap() for k, a in arrays.items()]
    out = nc.dram_tensor("out", w["x"].shape, F32, kind="ExternalOutput").ap()
    criss_cross_attention(nc, *args, out)
    r = run_bass_kernel_spmd(nc, [{f"in_{k}": a for k, a in arrays.items()}], core_ids=[0])
    return r.results[0]["out"]
```
